# Optimizing a Trainium2 kernel written in Bass

```python
import numpy as np
import jax
import jax.numpy as jnp

def _softmax(x, axis=-1):
    return jax.nn.softmax(x, axis=axis)

def _gelu(x):
    return jax.nn.gelu(x, approximate=True)

def _silu(x):
    return jax.nn.silu(x)

def _sigmoid(x):
    return jax.nn.sigmoid(x)

def _layernorm(x, axis=-1, eps=1e-05):
    m = jnp.mean(x, axis=axis, keepdims=True)
    v = jnp.var(x, axis=axis, keepdims=True)
    return (x - m) / jnp.sqrt(v + eps)

def _scatter_add(tgt, idx, src, axis=0):
    return tgt.at[idx].add(src)

def _segment_sum(src, seg, n):
    return jax.ops.segment_sum(src, seg, n)
kernel_name = 'mk_xattn_ffn_d1_seqx_r8_0bf208'

def setup_inputs(seed: int=0):
    np.random.seed(seed)
    _w = jnp.asarray

    def _rec_inputs():
        import jax
        import jax.numpy as jnp
        _rk = jax.random.key(seed)
        x = -0.0002928 + 1 * jax.random.normal(jax.random.fold_in(_rk, 1), (64, 64, 128), jnp.float32)
        _lenS = 64 - jax.random.randint(jax.random.fold_in(_rk, 7), (64,), 0, max(1, 64 // 4) + 1, jnp.int32)
        _lenS2 = 64 - jax.random.randint(jax.random.fold_in(_rk, 8), (64,), 0, max(1, 64 // 4) + 1, jnp.int32)
        _ctx_1024P = jax.random.normal(jax.random.fold_in(_rk, 11), (64, 16, 128), jnp.float32)
        _ctx_1024c = jax.random.dirichlet(jax.random.fold_in(_rk, 511), 0.3 * jnp.ones((16,), jnp.float32), (64, 64))
        _ctx_1024t = jnp.einsum('bsk,bkd->bsd', _ctx_1024c, _ctx_1024P)
        _ctx_1024t = _ctx_1024t * jax.lax.rsqrt(jnp.mean(jnp.square(_ctx_1024t)) + 1e-12) * 0.953939
        ctx_1024 = -1.39393e-06 + 0.999914 * (_ctx_1024t + 0.3 * jax.random.normal(jax.random.fold_in(_rk, 611), (64, 64, 128), jnp.float32))
        return (x, ctx_1024)
    x, ctx_1024 = _rec_inputs()

    def _L0_xattn_setup():
        import jax, jax.numpy as jnp
        import numpy as np
        D_MODEL = 128
        N_HEADS = 16
        D_K = D_MODEL // N_HEADS
        key = jax.random.key(seed)
        ks = jax.random.split(key, 12)
        B, S, D = (2, 256, D_MODEL)
        scale = 1.0 / np.sqrt(D)
        inp = {'q': jax.random.normal(ks[0], (B, S, D), jnp.float32), 'k': jax.random.normal(ks[1], (B, S, D), jnp.float32), 'v': jax.random.normal(ks[2], (B, S, D), jnp.float32), 'w_q': jax.random.normal(ks[3], (D, D), jnp.float32) * scale, 'b_q': jax.random.normal(ks[4], (D,), jnp.float32) * scale, 'w_k': jax.random.normal(ks[5], (D, D), jnp.float32) * scale, 'b_k': jax.random.normal(ks[6], (D,), jnp.float32) * scale, 'w_v': jax.random.normal(ks[7], (D, D), jnp.float32) * scale, 'b_v': jax.random.normal(ks[8], (D,), jnp.float32) * scale, 'w_o': jax.random.normal(ks[9], (D, D), jnp.float32) * scale, 'b_o': jax.random.normal(ks[10], (D,), jnp.float32) * scale}
        return inp
    _L0_xattn_all = _L0_xattn_setup()
    _L0_xattn_in = {k: v for k, v in _L0_xattn_all.items() if k in ('w_q', 'b_q', 'w_k', 'b_k', 'w_v', 'b_v', 'w_o', 'b_o')}
    del _L0_xattn_all

    def _L0_ffn_setup():
        import jax, jax.numpy as jnp
        import numpy as np
        import math
        D_IN = 128
        FEATURES = (512, 512, 128)
        BATCH, SEQ = (8, 256)

        def _conn_dense(kernel_bool, x):
            w = jnp.where(kernel_bool, jnp.float32(1.0), jnp.float32(-1.0))
            return x @ w
        key = jax.random.key(seed)
        kx, kk0, kk1, kk2 = jax.random.split(key, 4)
        x = jax.random.normal(kx, (BATCH, SEQ, D_IN), dtype=jnp.float32)
        k0 = jax.random.randint(kk0, (2 * D_IN, FEATURES[0]), 0, 2).astype(jnp.bool_)
        k1 = jax.random.randint(kk1, (FEATURES[0], FEATURES[1]), 0, 2).astype(jnp.bool_)
        k2 = jax.random.randint(kk2, (FEATURES[1], FEATURES[2]), 0, 2).astype(jnp.bool_)
        s0 = jnp.asarray(1.0 / math.sqrt(2 * D_IN), dtype=jnp.float32)
        s1 = jnp.asarray(1.0 / math.sqrt(FEATURES[0]), dtype=jnp.float32)
        s2 = jnp.asarray(1.0 / math.sqrt(FEATURES[1]), dtype=jnp.float32)
        return {'x': x, 'k0': k0, 'k1': k1, 'k2': k2, 's0': s0, 's1': s1, 's2': s2}
    _L0_ffn_all = _L0_ffn_setup()
    _L0_ffn_in = {k: v for k, v in _L0_ffn_all.items() if k in ('k0', 'k1', 'k2', 's0', 's1', 's2')}
    del _L0_ffn_all
    return {'x': x, 'ctx_1024': ctx_1024, 'L0_xattn_w_q': _L0_xattn_in['w_q'], 'L0_xattn_b_q': _L0_xattn_in['b_q'], 'L0_xattn_w_k': _L0_xattn_in['w_k'], 'L0_xattn_b_k': _L0_xattn_in['b_k'], 'L0_xattn_w_v': _L0_xattn_in['w_v'], 'L0_xattn_b_v': _L0_xattn_in['b_v'], 'L0_xattn_w_o': _L0_xattn_in['w_o'], 'L0_xattn_b_o': _L0_xattn_in['b_o'], 'L0_ffn_k0': _L0_ffn_in['k0'], 'L0_ffn_k1': _L0_ffn_in['k1'], 'L0_ffn_k2': _L0_ffn_in['k2'], 'L0_ffn_s0': _L0_ffn_in['s0'], 'L0_ffn_s1': _L0_ffn_in['s1'], 'L0_ffn_s2': _L0_ffn_in['s2']}

def reference(x, ctx_1024, L0_xattn_w_q, L0_xattn_b_q, L0_xattn_w_k, L0_xattn_b_k, L0_xattn_w_v, L0_xattn_b_v, L0_xattn_w_o, L0_xattn_b_o, L0_ffn_k0, L0_ffn_k1, L0_ffn_k2, L0_ffn_s0, L0_ffn_s1, L0_ffn_s2):
    import jax
    import jax.numpy as jnp

    def _L0_xattn_ref(q, k, v, w_q, b_q, w_k, b_k, w_v, b_v, w_o, b_o):
        import jax, jax.numpy as jnp
        import numpy as np
        D_MODEL = 128
        N_HEADS = 16
        D_K = D_MODEL // N_HEADS
        B, S, D = q.shape
        H, Dk = (N_HEADS, D_K)

        def proj(x, w, b):
            y = jnp.einsum('bsd,ed->bse', x, w) + b
            return y.reshape(B, S, H, Dk).transpose(0, 2, 1, 3)
        query = proj(q, w_q, b_q)
        key = proj(k, w_k, b_k)
        value = proj(v, w_v, b_v)
        scores = jnp.einsum('bhqd,bhkd->bhqk', query, key) / jnp.sqrt(jnp.asarray(Dk, query.dtype))
        attn = jax.nn.softmax(scores, axis=-1)
        x = jnp.einsum('bhqk,bhkd->bhqd', attn, value)
        x = x.transpose(0, 2, 1, 3).reshape(B, S, D)
        return jnp.einsum('bsd,ed->bse', x, w_o) + b_o

    def _L0_ffn_ref(x, k0, k1, k2, s0, s1, s2):
        import jax, jax.numpy as jnp
        import numpy as np
        import math
        D_IN = 128
        FEATURES = (512, 512, 128)
        BATCH, SEQ = (8, 256)

        def _conn_dense(kernel_bool, x):
            w = jnp.where(kernel_bool, jnp.float32(1.0), jnp.float32(-1.0))
            return x @ w
        h = jnp.concatenate([x, -x], axis=-1)
        h = s0 * _conn_dense(k0, h)
        h = jax.nn.relu(h) * 2
        h = s1 * _conn_dense(k1, h)
        h = jax.nn.relu(h) * 2
        h = s2 * _conn_dense(k2, h)
        return h
    x = x + _L0_xattn_ref(_layernorm(x, axis=-1), ctx_1024, ctx_1024, L0_xattn_w_q, L0_xattn_b_q, L0_xattn_w_k, L0_xattn_b_k, L0_xattn_w_v, L0_xattn_b_v, L0_xattn_w_o, L0_xattn_b_o)
    x = x + _L0_ffn_ref(_layernorm(x, axis=-1), L0_ffn_k0, L0_ffn_k1, L0_ffn_k2, L0_ffn_s0, L0_ffn_s1, L0_ffn_s2)
    return x

_drawn_inputs = setup_inputs


def setup_inputs(seed=0):
    import zlib

    import numpy as np

    out = dict(_drawn_inputs(seed))
    spreads = {}
    factors = {'L0_xattn_b_q': 2.852, 'L0_xattn_b_k': 8.0}
    for name, (base, spread) in spreads.items():
        noise = np.random.default_rng([zlib.crc32(name.encode()), seed]).standard_normal(out[name].shape)
        drawn = base * np.exp(spread * noise) if base else spread * noise
        out[name] = jnp.asarray(drawn.astype(out[name].dtype))
    for name, factor in factors.items():
        out[name] = (out[name] * factor).astype(out[name].dtype)
    return out
```

```python
from contextlib import ExitStack

import concourse.bass as bass
from concourse import mybir

F32 = mybir.dt.float32
F32R = mybir.dt.float32r
U8 = mybir.dt.uint8
U32 = mybir.dt.uint32
ALU = mybir.AluOpType
ACT = mybir.ActivationFunctionType
AX = mybir.AxisListType

P = 128
SEQ = 64
HEADS = 16
DH = P // HEADS
HP = HEADS // 2
G = 4
NB = 8
CH = NB * SEQ
HB = NB // 2
HT = CH // 2
TILES = CH // P
FF = 512
FM = FF // P
VC = DH + 1
OC = 2 * 2 * VC
EPS = 1e-5
SCALE = float(DH) ** -0.5

MISC = [
    ("out_t2", 2), ("pv3", 2), ("v1", 1), ("xn_t", 0), ("out_t3", 2), ("ctx_t", 0), ("q", 0), ("wo", 2), ("pv0", 1),
    ("k", 0), ("y0", 3), ("y1", 3), ("out_t0", 1), ("xn2_t", 2), ("pv1", 1), ("v0", 0), ("out_t1", 1), ("pv2", 1),
]
PLACE = {name: n for n, (name, _) in enumerate(MISC)}
LAG = 3


def program(nc, x, ctx_in, w_q, b_q, w_k, b_k, w_v, b_v, w_o, b_o, k0, k1, k2, s0, s1, s2, out, loop=False):
    chunks = x.shape[0] * x.shape[1] // CH
    turns = chunks + LAG
    x_v = x.rearrange("b s d -> (b s) d").rearrange("(c t p) d -> c p t d", t=TILES, p=P)
    ctx_v = ctx_in.rearrange("b s d -> (b s) d").rearrange("(c t p) d -> c p t d", t=TILES, p=P)
    out_v = out.rearrange("b s d -> (b s) d").rearrange("(c t p) d -> c p t d", t=TILES, p=P)
    q_scr = nc.dram_tensor("q_scr", [2, G, 2, 32, HT], F32, kind="Internal").ap()
    k_scr = nc.dram_tensor("k_scr", [2, 2, P, HT], F32, kind="Internal").ap()

    def live(c):
        return not isinstance(c, int) or 0 <= c < chunks

    def misc_bank(name):
        return PLACE[name] % 2

    def misc_turn(i, name):
        n = PLACE[name]

        def count(turn):
            return sum(live(t - lag) for t in range(turn + 1) for m, (_, lag) in enumerate(MISC)
                       if m % 2 == n % 2 and (t < turn or m < n))
        return count(i) if isinstance(i, int) else (i - LAG) * (len(MISC) // 2) + count(LAG)

    def misc_read(i, name):
        return misc_turn(i, name) + 1

    def wait(eng, sem, value):
        if not isinstance(value, int) or value > 0:
            eng.wait_ge(sem, value)

    with ExitStack() as stack:
        def sb(name, shape, dt=F32):
            return stack.enter_context(nc.sbuf_tensor(name, shape, dt))

        def bank(name):
            return stack.enter_context(nc.psum_tensor(name, [P, 512], F32))

        def sem(name):
            return stack.enter_context(nc.semaphore(name))

        x_all = sb("x_all", [P, chunks * TILES, P])
        ctx_sb = sb("ctx_sb", [P, TILES, P])
        xn = sb("xn", [P, TILES, P])
        xn_t = sb("xn_t", [P, CH])
        ctx_t = sb("ctx_t", [P, 2, SEQ * HB])
        q_parts = sb("q_parts", [P, 2, 2, HT], F32R)
        k_parts = sb("k_parts", [P, 2, 2, HT], F32R)
        q_st = [sb(f"q_st{n}", [P, G, HT], F32R) for n in range(2)]
        k_st = [sb(f"k_st{n}", [P, G, 4, HT], F32R) for n in range(2)]
        q_diag = [sb(f"q_diag{n}", [P, HB, 4, SEQ], F32R) for n in range(2)]
        k_grp = [sb(f"k_grp{n}", [P, G, HT], F32R) for n in range(2)]
        v_bd = [sb(f"v_bd{n}", [P, HB, HP, 2 * VC]) for n in range(2)]
        neg_max = [sb(f"neg_max{n}", [P, HP]) for n in range(2)]
        max_diag = [sb(f"max_diag{n}", [P, HP, SEQ], F32R) for n in range(2)]
        probs = [sb(f"probs{n}", [P, HP, P]) for n in range(2)]
        inv_den = [sb(f"inv_den{n}", [P, HP, 2]) for n in range(2)]
        attn = [sb(f"attn{n}", [P, HP, 2, DH]) for n in range(2)]
        attn_t = sb("attn_t", [P, CH])
        xn2 = sb("xn2", [P, TILES, P])
        xn2_t = sb("xn2_t", [P, 2, CH], F32R)
        h1 = sb("h1", [P, 2, FM, CH], F32R)
        h2 = sb("h2", [P, 2, FM, CH], F32R)
        st1, st2 = (sb(f"st{n}", [P, TILES, 6]) for n in (1, 2))
        mv1, mv2 = (sb(f"mv{n}", [P, TILES, 2]) for n in (1, 2))
        ve1, ve2 = (sb(f"ve{n}", [P, TILES]) for n in (1, 2))
        rs1, rs2 = (sb(f"rs{n}", [P, TILES]) for n in (1, 2))
        w_nat = sb("w_nat", [P, 4, P])
        wq_t, wk_t, wv_t, wo_t = (sb(f"{n}_t", [P, P]) for n in ("wq", "wk", "wv", "wo"))
        bq_c, bk_c, bv_c = (sb(f"b{n}_c", [P, 1]) for n in "qkv")
        bo_row = sb("bo_row", [P, P])
        bv_rep = sb("bv_rep", [P, P])
        k0_sb = sb("k0_sb", [P, 2, FF], U8)
        k1_sb = sb("k1_sb", [P, FM, FF], U8)
        k2_sb = sb("k2_sb", [P, FM, P], U8)
        w0d = xn2[:].rearrange("p t d -> p (t d)")
        w0 = sb("w0", [P, FF], F32R)
        w1 = sb("w1", [P, FM, FF], F32R)
        w2 = sb("w2", [P, FM, P], F32R)
        s_raw = sb("s_raw", [P, 3])
        s_pos, s_neg, s_sgn, s_sgn2, s_nsgn, s_abs = (
            sb(f"s_{n}", [P, 3]) for n in ("pos", "neg", "sgn", "sgn2", "nsgn", "abs"))
        s_a, s_b, s_fin = (sb(f"s_{n}", [P, 1]) for n in ("a", "b", "fin"))
        ident = sb("ident", [P, P])
        ident_q = sb("ident_q", [P, SEQ])
        ones = sb("ones", [P, P])
        same_half = sb("same_half", [P, P], F32R)
        g_mask = sb("g_mask", [P, G])
        minus_half = sb("minus_half", [P, TILES])

        score_ps = [bank(f"score_ps{n}") for n in range(2)]
        logit_ps = [bank(f"logit_ps{n}") for n in range(2)]
        ffn_ps = [bank(f"ffn_ps{n}") for n in range(2)]
        misc_ps = [bank(f"misc_ps{n}") for n in range(2)]

        in_w = sem("in_w")
        in_b = sem("in_b")
        in_k = sem("in_k")
        in_s = sem("in_s")
        ident_made = sem("ident_made")
        pool_const = sem("pool_const")
        dve_const = sem("dve_const")
        dve_step = sem("dve_step")
        zeroed_pool = sem("zeroed_pool")
        zeroed_dve = sem("zeroed_dve")
        w_turned = sem("w_turned")
        w_kept = sem("w_kept")
        bo_made = sem("bo_made")
        bv_made = sem("bv_made")
        bo_kept = sem("bo_kept")
        ffn_w_made = sem("ffn_w_made")
        x_in, ctx_in_s, out_done = sem("x_in"), sem("ctx_in_s"), sem("out_done")
        q_written, k_written = sem("q_written"), sem("k_written")
        q_diag_in = [sem(f"q_diag_in{n}") for n in range(2)]
        stacks_in = [sem(f"stacks_in{n}") for n in range(2)]
        st1_done, mv1_done, ve1_done, rs1_done, xn_done = (sem(n) for n in ("st1_done", "mv1_done", "ve1_done", "rs1_done", "xn_done"))
        x_biased = sem("x_biased")
        xn_turned, ctx_turned, q_made, q_hi, k_made, k_hi = (sem(n) for n in ("xn_turned", "ctx_turned", "q_made", "q_hi", "k_made", "k_hi"))
        v_made, k_grp_made = sem("v_made"), sem("k_grp_made")
        scores_made, max_made, diag_made = sem("scores_made"), sem("max_made"), sem("diag_made")
        logits_made, exp_done = sem("logits_made"), sem("exp_done")
        pv_made, den_done, attn_turned, wo_made = sem("pv_made"), sem("den_done"), sem("attn_turned"), sem("wo_made")
        st2_done, mv2_done, ve2_done, rs2_done, xn2_done = (sem(n) for n in ("st2_done", "mv2_done", "ve2_done", "rs2_done", "xn2_done"))
        xn2_turned, xn2_hi = sem("xn2_turned"), sem("xn2_hi")
        ffn_made, ffn_hi, ffn_lo = sem("ffn_made"), sem("ffn_hi"), sem("ffn_lo")
        y_made = sem("y_made")
        misc_free = [sem(f"misc_free{n}") for n in range(2)]

        block = stack.enter_context(nc.Block())

        def run(eng, body, stop=chunks):
            for i in range(LAG):
                body(i)
            if loop:
                with eng.Fori(LAG, stop) as i:
                    body(i)
            else:
                for i in range(LAG, stop):
                    body(i)
            for i in range(stop, turns):
                body(i)

        def kept(eng, i, name):
            eng.wait_ge(misc_free[misc_bank(name)], misc_read(i, name))

        @block.sync
        def _(sp):
            def load_x(c):
                dst = x_all[:, c * TILES:(c + 1) * TILES, :] if isinstance(c, int) else x_all[:, bass.ts(c, TILES), :]
                src = x_v[c] if isinstance(c, int) else x_v[bass.ds(c, 1)].rearrange("a p t d -> (a p) t d")
                sp.dma_start(dst, src).then_inc(x_in, 16)

            def load_ctx(c):
                src = ctx_v[c] if isinstance(c, int) else ctx_v[bass.ds(c, 1)].rearrange("a p t d -> (a p) t d")
                sp.dma_start(ctx_sb[:], src).then_inc(ctx_in_s, 16)

            def write_q(h):
                for v in range(2):
                    sp.dma_start(q_scr[h, :, v], q_parts[:, v, h, :].bitcast(F32)).then_inc(q_written, 16)

            def write_k(h):
                sp.dma_start(k_scr[h].rearrange("u r t -> r u t"), k_parts[:, :, h, :].bitcast(F32)).then_inc(k_written, 16)

            def load_q_diag(h):
                for h4 in range(G):
                    sp.dma_start(q_diag[h][32 * h4:32 * h4 + 32, :, h4, :].bitcast(F32),
                                 q_scr[h, h4, 0].rearrange("r (b q) -> r b q", b=HB)).then_inc(q_diag_in[h], 16)

            def load_stacks(h):
                for h4 in range(G):
                    src = q_scr[h, h4].rearrange("v (d g) t -> (v d) (g t)", g=G).unsqueeze(0).broadcast_to([2, 2 * DH, G * HT])
                    sp.dma_start(q_st[h][32 * h4:32 * h4 + 32].bitcast(F32), src).then_inc(stacks_in[h], 16)
                for h4 in range(G):
                    for u in range(2):
                        src = k_scr[h, u, 32 * h4:32 * h4 + 32].rearrange("(d g) t -> d g t", g=G).unsqueeze(0).broadcast_to([2, DH, G, HT])
                        r = 32 * h4 + 16 * u
                        sp.dma_start(k_st[h][r:r + 16, :, h4, :].bitcast(F32), src).then_inc(stacks_in[h], 16)

            load_x(0)
            load_ctx(0)
            for n, w in enumerate((w_q, w_k, w_v, w_o)):
                sp.dma_start(w_nat[:, n, :], w).then_inc(in_w, 16)
            for col, b in ((bq_c, b_q), (bk_c, b_k)):
                sp.dma_start(col[:], b.rearrange("(g h d e) -> h d g e", g=G, h=4, e=1),
                             allow_slow_non_contiguous=True).then_inc(in_b, 16)
            sp.dma_start(bv_c[:], b_v.rearrange("(p e) -> p e", e=1)).then_inc(in_b, 16)
            sp.dma_start(bo_row[:], b_o.partition_broadcast(P)).then_inc(in_b, 16)
            sp.dma_start(k0_sb[:], k0.rearrange("(c p) n -> p c n", p=P)).then_inc(in_k, 16)
            sp.dma_start(k1_sb[:], k1.rearrange("(c p) n -> p c n", p=P)).then_inc(in_k, 16)
            sp.dma_start(k2_sb[:], k2.rearrange("(c p) n -> p c n", p=P)).then_inc(in_k, 16)
            for n, s in enumerate((s0, s1, s2)):
                sp.dma_start(s_raw[:, n:n + 1], s.partition_broadcast(P)).then_inc(in_s, 16)

            def body(i):
                if live(i + 1):
                    wait(sp, x_in, 16 * (i + 1))
                    load_x(i + 1)
                if live(i - 1):
                    wait(sp, scores_made, NB * (i - 1))
                    load_q_diag(1)
                    wait(sp, logits_made, NB * (i - 1))
                    load_stacks(1)
                if live(i):
                    sp.wait_ge(ctx_turned, i + 1)
                    if live(i + 1):
                        load_ctx(i + 1)
                    if not isinstance(i, int) or i > 0:
                        for h in range(2):
                            sp.wait_ge(q_diag_in[h], 64 * i)
                            sp.wait_ge(stacks_in[h], 192 * i)
                    kept(sp, i, "q")
                    for h in range(2):
                        write_q(h)
                    kept(sp, i, "k")
                    for h in range(2):
                        write_k(h)
                    sp.wait_ge(q_written, 64 * (i + 1))
                    if isinstance(i, int) and i == 0:
                        sp.wait_ge(zeroed_dve, 1)
                    wait(sp, scores_made, NB * (i - 1) + HB)
                    load_q_diag(0)
                    wait(sp, logits_made, NB * (i - 1) + HB)
                    if isinstance(i, int) and i == 0:
                        sp.wait_ge(zeroed_pool, 2)
                    sp.wait_ge(k_written, 32 * (i + 1))
                    load_stacks(0)
                if live(i - 3):
                    c = i - 3
                    kept(sp, i, "y0")
                    kept(sp, i, "y1")
                    if isinstance(c, int):
                        sp.dma_start(out_v[c], x_all[:, c * TILES:(c + 1) * TILES, :]).then_inc(out_done, 16)
                    else:
                        sp.dma_start(out_v[bass.ds(c, 1)].rearrange("a p t d -> (a p) t d"),
                                     x_all[:, bass.ts(c, TILES), :]).then_inc(out_done, 16)

            run(sp, body, chunks - 1)
            sp.wait_ge(out_done, 16 * chunks)

        def tile_ap(c, t, n=1):
            if isinstance(c, int):
                return x_all[:, c * TILES + t:c * TILES + t + n, :]
            return x_all[:, bass.ds(c * TILES + t, n), :]

        @block.tensor
        def _(pe):
            def misc(i, name):
                wait(pe, misc_free[misc_bank(name)], misc_turn(i, name))
                return misc_ps[misc_bank(name)]

            def scores(c, b):
                h, n = b // HB, b % HB
                if n == 0:
                    pe.wait_ge(q_diag_in[h], 64 * (c + 1))
                    pe.wait_ge(k_grp_made, 2 * c + h + 1)
                wait(pe, max_made, NB * c + b - 1)
                for hp in range(HP):
                    g, j = divmod(hp, 2)
                    mm = pe.matmul(score_ps[b % 2][:, hp * SEQ:(hp + 1) * SEQ],
                                   q_diag[h][:, n, 2 * j:2 * j + 2, :], k_grp[h][:, g, n * SEQ:(n + 1) * SEQ],
                                   start=True, stop=True)
                mm.then_inc(scores_made, 1)

            def logits(c, b):
                h, n = b // HB, b % HB
                if n == 0:
                    pe.wait_ge(stacks_in[h], 192 * (c + 1))
                wait(pe, exp_done, NB * c + b - 1)
                for hp in range(HP):
                    g, j = divmod(hp, 2)
                    w = k_st[h][:, g, 2 * j:2 * j + 2, :].rearrange("p h (k b) -> p b (h k)", b=HB)[:, n, :]
                    pe.matmul(logit_ps[b % 2][:, hp * SEQ:(hp + 1) * SEQ], w, q_st[h][:, g, n * SEQ:(n + 1) * SEQ],
                              start=(hp == 0), stop=False, skip_group_check=True)
                pe.wait_ge(diag_made, NB * c + b + 1)
                pe.matmul(logit_ps[b % 2][:], same_half[:], max_diag[b % 2][:].rearrange("p a b -> p (a b)"),
                          start=False, stop=True, skip_group_check=True).then_inc(logits_made, 1)

            def values(i, c, p):
                h = p // 2
                pe.wait_ge(exp_done, NB * c + 2 * p + 2)
                kept(pe, c + h, f"v{h}")
                o = misc(i, f"pv{p}")
                n = 2 * (p % 2)
                for hp in range(HP):
                    mm = pe.matmul(o[:, hp * OC:(hp + 1) * OC].rearrange("p (b c) -> p b c", b=2), probs[p % 2][:, hp, :], v_bd[h][:, n:n + 2, hp, :],
                                   start=True, stop=True)
                mm.then_inc(pv_made, 1)

            def turn_attn(i, c, p):
                kept(pe, c + 1 + (p == 3), f"pv{p}")
                o = misc(i, f"out_t{p}")
                pe.transpose(o[:, 0:P], attn[p % 2][:].rearrange("p a b d -> p (a b d)"), ident[:]).then_inc(attn_turned, 1)

            def turn(src, dst, done):
                for t in range(TILES):
                    mm = pe.transpose(dst[:, t * P:(t + 1) * P], src[:, t, :], ident[:])
                mm.then_inc(done, 1)

            def project_v(i, c, h):
                kept(pe, c, "ctx_t")
                o = misc(i, f"v{h}")
                w = wv_t[:].rearrange("m (a b d) -> m b a d", b=2, d=DH)
                for n in range(HB):
                    keys = ctx_t[:, h, :].rearrange("p (k b) -> p b k", b=HB)[:, n, :]
                    for r in range(2):
                        mm = pe.matmul(o[r * SEQ:(r + 1) * SEQ, n * SEQ:(n + 1) * SEQ].rearrange("p (a d) -> p a d", d=DH), keys, w[:, r], start=True, stop=True)
                mm.then_inc(v_made, 1)

            def layer1(c, m):
                if m == 0:
                    pe.wait_ge(ffn_lo, 2 * FM * c + FM)
                ffn_tile(c, FM + m, [(w1[:, k, m * P:(m + 1) * P], h1[:, part, k, :]) for k in range(FM) for part in range(2)])

            def ffn_tile(c, f, pairs):
                wait(pe, ffn_lo, 2 * FM * c + f - 1)
                for n, (w, a) in enumerate(pairs):
                    mm = pe.matmul(ffn_ps[f % 2][:], w, a, start=(n == 0), stop=(n == len(pairs) - 1))
                mm.then_inc(ffn_made, 1)

            def layer2(i, c, half):
                pe.wait_ge(ffn_lo, 2 * FM * (c + 1))
                o = misc(i, f"y{half}")
                for t in range(2):
                    tok = (2 * half + t) * P
                    for k in range(FM):
                        for part in range(2):
                            mm = pe.matmul(o[:, t * P:(t + 1) * P], h2[:, part, k, tok:tok + P], w2[:, k, :],
                                           start=(k == 0 and part == 0), stop=(k == FM - 1 and part == 1))
                mm.then_inc(y_made, 1)

            pe.wait_ge(ident_made, 1)
            pe.wait_ge(in_w, 64)
            for n in range(4):
                mm = pe.transpose(ffn_ps[0][:, n * P:(n + 1) * P], w_nat[:, n, :], ident[:])
            mm.then_inc(w_turned, 1)

            def body(i):
                c = i - 1
                for s in range(NB):
                    if live(c):
                        scores(c, s)
                    if s < 2 and live(i - 3):
                        layer1(i - 3, 1 + s)
                    if s == 2:
                        if live(i - 1):
                            project_v(i, i - 1, 1)
                        if live(i):
                            pe.wait_ge(xn_done, i + 1)
                            turn(xn, misc(i, "xn_t"), xn_turned)
                        if live(i - 3):
                            layer1(i - 3, 3)
                    if s == 3:
                        if live(i):
                            pe.wait_ge(ctx_in_s, 16 * (i + 1))
                            turn(ctx_sb, misc(i, "ctx_t"), ctx_turned)
                            kept(pe, i, "xn_t")
                            if isinstance(i, int) and i == 0:
                                pe.wait_ge(w_kept, 4)
                            pe.matmul(misc(i, "q")[:], wq_t[:], xn_t[:], start=True, stop=True).then_inc(q_made, 1)
                        if live(i - 2):
                            for p in range(4):
                                kept(pe, i - (p < 2), f"out_t{p}")
                            o = misc(i, "wo")
                            for t in range(TILES):
                                mm = pe.matmul(o[:, t * P:(t + 1) * P], attn_t[:, t * P:(t + 1) * P], wo_t[:], start=True, stop=True)
                            mm.then_inc(wo_made, 1)
                    if s == 4:
                        if live(i):
                            kept(pe, i, "ctx_t")
                            pe.matmul(misc(i, "k")[:], wk_t[:], ctx_t[:].rearrange("p h t -> p (h t)"),
                                      start=True, stop=True).then_inc(k_made, 1)
                            if isinstance(i, int) and i == 0:
                                pe.wait_ge(bv_made, 1)
                                pe.matmul(ffn_ps[1][:, 0:P], bv_rep[:], wo_t[:], start=True, stop=True).then_inc(bo_made, 1)
                        if live(i - 3):
                            layer2(i, i - 3, 0)
                            layer2(i, i - 3, 1)
                    if s == 5 and live(i - 2):
                        pe.wait_ge(xn2_done, i - 1)
                        turn(xn2, misc(i, "xn2_t"), xn2_turned)
                    if s == 6:
                        if live(i):
                            project_v(i, i, 0)
                        if live(i - 2):
                            kept(pe, i, "xn2_t")
                            if isinstance(i, int) and i == 2:
                                pe.wait_ge(ffn_w_made, 1)
                                pe.wait_ge(bo_kept, 1)
                            for m in range(FM):
                                ffn_tile(i - 2, m, [(w0[:, m * P:(m + 1) * P], xn2_t[:, part, :]) for part in range(2)])
                    if s == 7 and live(i - 2):
                        layer1(i - 2, 0)
                    if s > 0 and live(c):
                        logits(c, s - 1)
                    if s == 0 and live(c - 1):
                        logits(c - 1, NB - 1)
                    if s == 1 and live(i - 2):
                        values(i, i - 2, 3)
                    if s in (3, 5, 7) and live(i - 1):
                        values(i, i - 1, (s - 3) // 2)
                    if s in (0, 2) and live(i - 2):
                        turn_attn(i, i - 2, 2 + s // 2)
                    if s in (4, 6) and live(i - 1):
                        turn_attn(i, i - 1, (s - 4) // 2)

            run(pe, body)

        @block.scalar
        def _(act):
            def hi_ffn(c, f):
                h, m = (h1, f) if f < FM else (h2, f - FM)
                act.wait_ge(ffn_made, 2 * FM * c + f + 1)
                act.activation(h[:, 0, m, :], ffn_ps[f % 2][:], ACT.Relu).then_inc(ffn_hi, 1)

            def exp(c, b):
                p, r = divmod(b, 2)
                act.wait_ge(logits_made, NB * c + b + 1)
                if r == 0:
                    wait(act, pv_made, 4 * c + p - 1)
                act.activation(probs[p % 2][:, :, r * SEQ:(r + 1) * SEQ],
                               logit_ps[b % 2][:].rearrange("p (a q) -> p a q", a=HP), ACT.Exp, scale=SCALE).then_inc(exp_done, 1)

            def keep_v(c, h):
                act.wait_ge(v_made, 2 * c + h + 1)
                wait(act, pv_made, 4 * (c - 1) + 2 * (h + 1))
                if isinstance(c, int) and c == 0:
                    act.wait_ge(zeroed_dve, 3)
                src = misc_ps[misc_bank(f"v{h}")][:, 0:HB * SEQ].rearrange("p (b a d) -> p b a d", b=HB, d=DH)
                for r in range(2):
                    rows = slice(r * SEQ, (r + 1) * SEQ)
                    cp = act.copy(v_bd[h][rows, :, :, r * VC:r * VC + DH], src[rows])
                cp.then_inc(misc_free[misc_bank(f"v{h}")], 1)

            def keep_attn_t(c, p):
                act.wait_ge(attn_turned, 4 * c + p + 1)
                if p == 0:
                    wait(act, wo_made, c)
                n = misc_bank(f"out_t{p}")
                act.copy(attn_t[:, p * P:(p + 1) * P], misc_ps[n][:, 0:P]).then_inc(misc_free[n], 1)

            act.wait_ge(w_turned, 1)
            for n, w in enumerate((wq_t, wk_t)):
                act.copy(w[:].rearrange("p (h d g) -> p g h d", h=4, g=G),
                         ffn_ps[0][:, n * P:(n + 1) * P].rearrange("p (g h d) -> p g h d", g=G, h=4)).then_inc(w_kept, 1)
            for n, w in enumerate((wv_t, wo_t)):
                act.copy(w[:], ffn_ps[0][:, (n + 2) * P:(n + 3) * P]).then_inc(w_kept, 1)
            act.wait_ge(in_b, 64)

            def body(i):
                for s in range(NB):
                    if s < 3:
                        if s == 2:
                            if live(i - 1):
                                keep_v(i - 1, 1)
                            if live(i):
                                act.wait_ge(xn_turned, i + 1)
                                wait(act, q_made, i)
                                act.copy(xn_t[:], misc_ps[misc_bank("xn_t")][:]).then_inc(misc_free[misc_bank("xn_t")], 1)
                        if live(i - 3):
                            hi_ffn(i - 3, FM + 1 + s)
                    if s == 3 and live(i):
                        act.wait_ge(ctx_turned, i + 1)
                        if not isinstance(i, int) or i > 0:
                            act.wait_ge(v_made, 2 * i)
                        n = misc_bank("ctx_t")
                        act.copy(ctx_t[:].rearrange("p h (k b) -> p h b k", b=HB),
                                 misc_ps[n][:].rearrange("p (h b k) -> p h b k", h=2, b=HB)).then_inc(misc_free[n], 1)
                        act.wait_ge(q_made, i + 1)
                        wait(act, q_written, 64 * i)
                        act.activation(q_parts[:, 0].rearrange("p h t -> p (h t)"), misc_ps[misc_bank("q")][:], ACT.Identity,
                                       bias=bq_c[:, 0:1]).then_inc(q_hi, 1)
                    if s == 4 and live(i):
                        act.wait_ge(k_made, i + 1)
                        wait(act, k_written, 32 * i)
                        wait(act, k_grp_made, 2 * i)
                        act.activation(k_parts[:, 0].rearrange("p h t -> p (h t)"), misc_ps[misc_bank("k")][:], ACT.Identity,
                                       bias=bk_c[:, 0:1]).then_inc(k_hi, 1)
                    if s == 5 and live(i - 2):
                        act.wait_ge(xn2_turned, i - 1)
                        wait(act, ffn_made, 2 * FM * (i - 3) + FM)
                        act.copy(xn2_t[:, 0, :], misc_ps[misc_bank("xn2_t")][:]).then_inc(xn2_hi, 1)
                    if s == 6:
                        if live(i):
                            keep_v(i, 0)
                        if live(i - 2):
                            for m in range(FM):
                                hi_ffn(i - 2, m)
                    if s == 7 and live(i - 2):
                        hi_ffn(i - 2, FM)
                    if s > 0 and live(i - 1):
                        exp(i - 1, s - 1)
                    if s == 0 and live(i - 2):
                        exp(i - 2, NB - 1)
                    if s in (0, 2) and live(i - 2):
                        keep_attn_t(i - 2, 2 + s // 2)
                    if s in (4, 6) and live(i - 1):
                        keep_attn_t(i - 1, (s - 4) // 2)

            run(act, body)

        @block.gpsimd
        def _(pool):
            pool.memset(ones[:], 1.0).then_inc(pool_const, 1)
            pool.wait_ge(pool_const, 1)
            pool.affine_select(out=ident[:], in_=ones[:], compare_op=ALU.is_equal, fill=0.0, base=0,
                               pattern=[[-1, P]], channel_multiplier=1).then_inc(ident_made, 1)
            pool.memset(minus_half[:], -0.5).then_inc(pool_const, 1)
            for h in range(2):
                pool.memset(k_st[h][:].bitcast(U32), 0).then_inc(zeroed_pool, 1)

            def rstd(mv, ve, rs, mv_done, ve_done, rs_done, c):
                pool.wait_ge(mv_done, c + 1)
                pool.tensor_scalar(ve[:], mv[:, :, 1], EPS, None, ALU.add).then_inc(ve_done, 1)
                pool.wait_ge(ve_done, c + 1)
                pool.tensor_tensor(rs[:], ve[:], minus_half[:], ALU.pow).then_inc(rs_done, 1)

            def group_keys(c, h, gs):
                if gs[0] == 0:
                    pool.wait_ge(k_hi, c + 1)
                    wait(pool, scores_made, NB * (c - 1) + HB * (h + 1))
                for g in gs:
                    op = pool.tensor_scalar(k_grp[h][:, g, :].rearrange("p (b k) -> p b k", b=HB),
                                            k_parts[:, 0, h, :].bitcast(F32).rearrange("p (k b) -> p b k", b=HB),
                                            g_mask[:, g:g + 1], 1.0, ALU.mult, ALU.mult)
                if gs[-1] == G - 1:
                    op.then_inc(k_grp_made, 1)

            def diag(c, b):
                pool.wait_ge(max_made, NB * c + b + 1)
                wait(pool, logits_made, NB * c + b - 1)
                pool.tensor_tensor(max_diag[b % 2][:], ident_q[:].unsqueeze(1).broadcast_to([P, HP, SEQ]),
                                   neg_max[b % 2][:].unsqueeze(2).broadcast_to([P, HP, SEQ]), ALU.mult).then_inc(diag_made, 1)

            pool.wait_ge(dve_const, 3)

            def body(i):
                for s in range(NB):
                    if s == 0:
                        if live(i):
                            rstd(mv1, ve1, rs1, mv1_done, ve1_done, rs1_done, i)
                        if live(i - 1):
                            group_keys(i - 1, 1, (0, 1))
                    if s == 1 and live(i - 1):
                        group_keys(i - 1, 1, (2, 3))
                    if s == 2 and live(i):
                        pool.wait_ge(xn_done, i + 1)
                        pool.wait_ge(bo_kept, 1) if not isinstance(i, int) or i == 0 else None
                        xa = tile_ap(i, 0, TILES)
                        pool.tensor_tensor(xa, xa, bo_row[:].unsqueeze(1).broadcast_to([P, TILES, P]), ALU.add).then_inc(x_biased, 1)
                    if s == 3 and live(i - 2):
                        rstd(mv2, ve2, rs2, mv2_done, ve2_done, rs2_done, i - 2)
                    if s == 5 and live(i):
                        group_keys(i, 0, (0, 1))
                    if s == 6 and live(i):
                        group_keys(i, 0, (2, 3))
                    if live(i - 1):
                        diag(i - 1, s)

            run(pool, body)

        @block.vector
        def _(dve):
            def stats(c, st, mv, st_done, mv_done, x_ready=None):
                if x_ready:
                    dve.wait_ge(*x_ready)
                for t in range(TILES):
                    op = dve.bn_stats(st[:, t, :], tile_ap(c, t).rearrange("p t d -> p (t d)"))
                op.then_inc(st_done, 1)
                dve.wait_ge(st_done, c + 1)
                for t in range(TILES):
                    op = dve.bn_aggr(mv[:, t, :], st[:, t, :])
                op.then_inc(mv_done, 1)

            def normalise(c, dst, mv, rs, rs_done, done, free):
                dve.wait_ge(rs_done, c + 1)
                wait(dve, *free)
                for t in range(TILES):
                    op = dve.tensor_scalar(dst[:, t, :], tile_ap(c, t).rearrange("p t d -> p (t d)"), mv[:, t, 0:1], rs[:, t:t + 1],
                                           ALU.subtract, ALU.mult)
                op.then_inc(done, 1)

            def row_max(c, b):
                dve.wait_ge(scores_made, NB * c + b + 1)
                wait(dve, diag_made, NB * c + b - 1)
                dve.tensor_reduce(neg_max[b % 2][:], score_ps[b % 2][:].rearrange("p (a k) -> p a k", a=HP), AX.X, ALU.max,
                                  negate=True).then_inc(max_made, 1)

            def lo_ffn(c, f):
                h, m = (h1, f) if f < FM else (h2, f - FM)
                dve.wait_ge(ffn_hi, 2 * FM * c + f + 1)
                dve.scalar_tensor_tensor(out=h[:, 1, m, :], in0=ffn_ps[f % 2][:], scalar=0.0, in1=h[:, 0, m, :].bitcast(F32),
                                         op0=ALU.max, op1=ALU.subtract).then_inc(ffn_lo, 1)

            def lo_part(parts, name, hi_sem, c, bias):
                dve.wait_ge(hi_sem, c + 1)
                n = misc_bank(name)
                dve.scalar_tensor_tensor(out=parts[:, 1].rearrange("p h t -> p (h t)") if parts is not xn2_t else parts[:, 1],
                                         in0=misc_ps[n][:], scalar=bias,
                                         in1=(parts[:, 0].rearrange("p h t -> p (h t)") if parts is not xn2_t else parts[:, 0]).bitcast(F32),
                                         op0=ALU.add, op1=ALU.subtract).then_inc(misc_free[n], 1)

            def normalise_attn(c, p):
                dve.wait_ge(pv_made, 4 * c + p + 1)
                wait(dve, attn_turned, 4 * c + p - 1)
                n = misc_bank(f"pv{p}")
                o = misc_ps[n][:, 0:HP * OC].rearrange("p (a b r c) -> p b a r c", a=HP, b=2, r=2)
                for r in range(2):
                    rows = slice(r * SEQ, (r + 1) * SEQ)
                    op = dve.reciprocal(inv_den[p % 2][rows], o[rows, r, :, :, DH])
                op.then_inc(den_done, 1)
                dve.wait_ge(den_done, 4 * c + p + 1)
                for r in range(2):
                    rows = slice(r * SEQ, (r + 1) * SEQ)
                    op = dve.tensor_tensor(attn[p % 2][rows], o[rows, r, :, :, 0:DH],
                                           inv_den[p % 2][rows].unsqueeze(3).broadcast_to([SEQ, HP, 2, DH]), ALU.mult)
                op.then_inc(misc_free[n], 1)

            dve.memset(q_diag[0][:].bitcast(U32), 0).then_inc(zeroed_dve, 1)
            dve.memset(q_diag[1][:].bitcast(U32), 0)
            dve.wait_ge(ident_made, 1)
            dve.tensor_tensor(ident_q[:], ident[:, 0:SEQ], ident[:, SEQ:P], ALU.add).then_inc(dve_const, 1)
            dve.tensor_reduce(g_mask[:], ident[:].rearrange("p (a g) -> p g a", g=G), AX.X, ALU.add).then_inc(dve_const, 1)
            for r in range(2):
                rows = slice(r * SEQ, (r + 1) * SEQ)
                for q in range(2):
                    dve.tensor_scalar(same_half[rows, q * SEQ:(q + 1) * SEQ], ones[rows, 0:SEQ], 1.0 if q == r else 0.0, None, ALU.mult)
            dve.tensor_copy(s_abs[:, 0:1], ones[:, 0:1]).then_inc(dve_const, 1)
            dve.memset(v_bd[0][:].bitcast(U32), 0)
            dve.memset(v_bd[1][:].bitcast(U32), 0).then_inc(zeroed_dve, 1)
            dve.wait_ge(zeroed_dve, 2)
            for n in range(2):
                for r in range(2):
                    op = dve.memset(v_bd[n][r * SEQ:(r + 1) * SEQ, :, :, r * VC + DH:r * VC + DH + 1], 1.0)
            op.then_inc(zeroed_dve, 1)
            step = 0

            def chain(op):
                nonlocal step
                step += 1
                op.then_inc(dve_step, 1)
                dve.wait_ge(dve_step, step)

            def setup_ffn():
                dve.wait_ge(in_s, 48)
                dve.wait_ge(in_k, 48)
                dve.tensor_scalar(s_pos[:], s_raw[:], 0.0, None, ALU.is_gt)
                chain(dve.tensor_scalar(s_neg[:], s_raw[:], 0.0, None, ALU.is_lt))
                chain(dve.tensor_tensor(s_sgn[:], s_pos[:], s_neg[:], ALU.subtract))
                dve.tensor_scalar(s_sgn2[:], s_sgn[:], 2.0, None, ALU.mult)
                dve.tensor_scalar(s_nsgn[:], s_sgn[:], -1.0, None, ALU.mult)
                dve.tensor_tensor(w0d, k0_sb[:, 0, :], k0_sb[:, 1, :], ALU.subtract)
                chain(dve.tensor_tensor(s_abs[:], s_raw[:], s_sgn[:], ALU.mult))
                dve.tensor_scalar(w0[:], w0d, s_sgn2[:, 0:1], None, ALU.mult)
                dve.tensor_scalar(w1[:], k1_sb[:], s_sgn2[:, 1:2], s_nsgn[:, 1:2], ALU.mult, ALU.add)
                dve.tensor_scalar(w2[:], k2_sb[:], 2.0, -1.0, ALU.mult, ALU.add)
                chain(dve.tensor_tensor(s_a[:], s_abs[:, 0:1], s_abs[:, 1:2], ALU.mult))
                chain(dve.tensor_scalar(s_b[:], s_a[:], 4.0, None, ALU.mult))
                chain(dve.tensor_tensor(s_fin[:], s_b[:], s_raw[:, 2:3], ALU.mult))
                dve.tensor_copy(s_a[:], s_fin[:]).then_inc(ffn_w_made, 1)

            def body(i):
                for s in range(NB):
                    if live(i - 1):
                        row_max(i - 1, s)
                    if s == 0 and live(i):
                        stats(i, st1, mv1, st1_done, mv1_done, (x_in, 16 * (i + 1)))
                    if s == 1 and live(i):
                        normalise(i, xn, mv1, rs1, rs1_done, xn_done, (xn_turned, i))
                        if isinstance(i, int) and i == 0:
                            dve.wait_ge(in_b, 64)
                            dve.tensor_scalar(bv_rep[:], ones[:], bv_c[:, 0:1], None, ALU.mult).then_inc(bv_made, 1)
                    if s < 3 and live(i - 3):
                        lo_ffn(i - 3, FM + 1 + s)
                    if s == 3:
                        if live(i):
                            lo_part(q_parts, "q", q_hi, i, bq_c[:, 0:1])
                        if live(i - 2):
                            dve.wait_ge(wo_made, i - 1)
                            dve.wait_ge(x_biased, i - 1)
                            xa = tile_ap(i - 2, 0, TILES)
                            n = misc_bank("wo")
                            dve.tensor_tensor(xa, misc_ps[n][:].rearrange("p (t d) -> p t d", t=TILES), xa, ALU.add).then_inc(misc_free[n], 1)
                            stats(i - 2, st2, mv2, st2_done, mv2_done, (misc_free[n], misc_read(i, "wo")))
                    if s == 4:
                        if live(i):
                            lo_part(k_parts, "k", k_hi, i, bk_c[:, 0:1])
                            if isinstance(i, int) and i == 0:
                                dve.wait_ge(bo_made, 1)
                                dve.tensor_tensor(bo_row[:], ffn_ps[1][:, 0:P], bo_row[:], ALU.add).then_inc(bo_kept, 1)
                                setup_ffn()
                        if live(i - 2):
                            normalise(i - 2, xn2, mv2, rs2, rs2_done, xn2_done, (xn2_turned, i - 2))
                        if live(i - 3):
                            for half in range(2):
                                n = misc_bank(f"y{half}")
                                dve.wait_ge(y_made, 2 * (i - 3) + half + 1)
                                xa = tile_ap(i - 3, 2 * half, 2).rearrange("p t d -> p (t d)")
                                dve.scalar_tensor_tensor(out=xa, in0=misc_ps[n][:, 0:2 * P], scalar=s_fin[:, 0:1], in1=xa,
                                                         op0=ALU.mult, op1=ALU.add).then_inc(misc_free[n], 1)
                    if s == 5 and live(i - 2):
                        lo_part(xn2_t, "xn2_t", xn2_hi, i - 2, 0.0)
                    if s == 6 and live(i - 2):
                        for m in range(FM):
                            lo_ffn(i - 2, m)
                    if s == 7 and live(i - 2):
                        lo_ffn(i - 2, FM)
                    if s == 1 and live(i - 2):
                        normalise_attn(i - 2, 3)
                    if s in (3, 5, 7) and live(i - 1):
                        normalise_attn(i - 1, (s - 3) // 2)

            run(dve, body)
    return nc


_INS = ['x', 'ctx_1024', 'L0_xattn_w_q', 'L0_xattn_b_q', 'L0_xattn_w_k', 'L0_xattn_b_k', 'L0_xattn_w_v', 'L0_xattn_b_v',
        'L0_xattn_w_o', 'L0_xattn_b_o', 'L0_ffn_k0', 'L0_ffn_k1', 'L0_ffn_k2', 'L0_ffn_s0', 'L0_ffn_s1', 'L0_ffn_s2']


def kernel(**inputs):
    import numpy as _np
    import concourse.bacc as _bacc
    from concourse import mybir as _mybir
    from concourse.bass_utils import run_bass_kernel_spmd as _run

    nc = _bacc.Bacc("TRN2", target_bir_lowering=False, num_devices=1)
    arrays, args = {}, []
    for name in _INS:
        a = _np.ascontiguousarray(inputs[name])
        if a.ndim == 0:
            a = a.reshape(1)
        arrays[f"in_{name}_dram"] = a
        args.append(nc.dram_tensor(f"in_{name}_dram", a.shape, _mybir.dt.from_np(a.dtype), kind="ExternalInput").ap())
    shape = tuple(_np.shape(inputs['x']))
    args.append(nc.dram_tensor("out_0_dram", shape, _mybir.dt.float32, kind="ExternalOutput").ap())
    program(nc, *args)
    r = _run(nc, [arrays], core_ids=[0])
    return r.results[0]["out_0_dram"]
```

```python
from contextlib import ExitStack

import concourse.bass as bass
from concourse import mybir

F32 = mybir.dt.float32
F32R = mybir.dt.float32r
U8 = mybir.dt.uint8
U32 = mybir.dt.uint32
ALU = mybir.AluOpType
ACT = mybir.ActivationFunctionType
AX = mybir.AxisListType

P = 128
SEQ = 64
HEADS = 16
DH = P // HEADS
HP = HEADS // 2
G = 4
NB = 4
CH = NB * SEQ
TILES = CH // P
UNITS = 2 * TILES
UH = HEADS // 2
SLOTS = UNITS
FF = 512
FM = FF // P
FT = 2 * FM // 2
VC = DH + 1
OC = 2 * 2 * VC
EPS = 1e-5
SCALE = float(DH) ** -0.5
LAG = 4

MISC = [
    ("front_t", 0, 1), ("out_t1", 3, 0), ("wo", 3, 0), ("qk", 0, 1), ("pv0", 2, 0), ("out_t0", 2, 0),
    ("xn2_t", 3, 1), ("y_t", 4, 0), ("y", 4, 1), ("pv1", 2, 0), ("v", 0, 1),
]
LOADS = [(0, 1, None), (1, 3, None), (3, 8, 1), (8, 16, 2)]


def program(nc, x, ctx_in, w_q, b_q, w_k, b_k, w_v, b_v, w_o, b_o, k0, k1, k2, s0, s1, s2, out):
    chunks = x.shape[0] * x.shape[1] // CH
    turns = chunks + LAG
    x_v = x.rearrange("b s d -> (b s) d").rearrange("(t p) d -> p t d", p=P)
    ctx_v = ctx_in.rearrange("b s d -> (b s) d").rearrange("(t p) d -> p t d", p=P)
    out_v = out.rearrange("b s d -> (b s) d").rearrange("(t p) d -> p t d", p=P)
    q_scr = nc.dram_tensor("q_scr", [2, G, 2, 2, DH * G, CH], F32, kind="Internal").ap()
    k_scr = nc.dram_tensor("k_scr", [2, G, 2, DH * G, CH], F32, kind="Internal").ap()

    def live(c):
        return 0 <= c < chunks

    def misc_lag_bank(name):
        return next((lag, b) for n, lag, b in MISC if n == name)

    def misc_used(name, c):
        lag, bank_no = misc_lag_bank(name)
        turn, place = c + lag, [n for n, _, _ in MISC].index(name)
        return sum(live(t - l) for t in range(turn + 1) for m, (_, l, b) in enumerate(MISC)
                   if b == bank_no and (t < turn or m < place))

    def wait(eng, sem, value):
        if value > 0:
            eng.wait_ge(sem, value)

    with ExitStack() as stack:
        def sb(name, shape, dt=F32):
            return stack.enter_context(nc.sbuf_tensor(name, shape, dt))

        def bank(name):
            return stack.enter_context(nc.psum_tensor(name, [P, 512], F32))

        def sem(name):
            return stack.enter_context(nc.semaphore(name))

        x_all = sb("x_all", [P, chunks * TILES, P])
        ctx_all = sb("ctx_all", [P, chunks * TILES, P])
        xn = sb("xn", [P, TILES, P])
        front = sb("front", [P, 2, CH])
        parts = sb("parts", [P, 2, 2, CH], F32R)
        q_st = [sb(f"q_st{n}", [P, G, NB, 2 * SEQ], F32R) for n in range(2)]
        k_st = [sb(f"k_st{n}", [P, G, 4, CH], F32R) for n in range(2)]
        v_bd = [sb(f"v_bd{n}", [P, NB, HP, 2 * VC]) for n in range(2)]
        row_max = [sb(f"row_max{n}", [P, UH]) for n in range(2)]
        shifted = [sb(f"shifted{n}", [P, UH * SEQ]) for n in range(2)]
        probs = [sb(f"probs{n}", [P, UH // 2, P]) for n in range(UNITS)]
        inv_den = [sb(f"inv_den{n}", [P, HP, 2]) for n in range(TILES)]
        attn = [sb(f"attn{n}", [P, HP, 2, DH]) for n in range(TILES)]
        attn_t = sb("attn_t", [P, CH])
        xn2 = sb("xn2", [P, TILES, P])
        xn2_t = sb("xn2_t", [P, 2, CH], F32R)
        h1 = sb("h1", [P, 2, FM, CH], F32R)
        h2 = sb("h2", [P, 2, FM, CH], F32R)
        y_t = sb("y_t", [P, CH])
        st1, st2 = (sb(f"st{n}", [P, TILES, 6]) for n in (1, 2))
        mv1, mv2 = (sb(f"mv{n}", [P, TILES, 2]) for n in (1, 2))
        ve1, ve2 = (sb(f"ve{n}", [P, TILES]) for n in (1, 2))
        rs1, rs2 = (sb(f"rs{n}", [P, TILES]) for n in (1, 2))
        w_nat = sb("w_nat", [P, 4, P])
        wq_t, wk_t, wv_t, wo_t = (sb(f"{n}_t", [P, P]) for n in ("wq", "wk", "wv", "wo"))
        bq_c, bk_c, bv_c = (sb(f"b{n}_c", [P, 1]) for n in "qkv")
        bo_row = sb("bo_row", [P, P])
        bv_rep = sb("bv_rep", [P, P])
        k0_sb = sb("k0_sb", [P, 2, FF], U8)
        k1_sb = sb("k1_sb", [P, FM, FF], U8)
        k2_sb = sb("k2_sb", [P, FM, P], U8)
        k0_diff = sb("k0_diff", [P, FF])
        w0 = sb("w0", [P, FF], F32R)
        w1 = sb("w1", [P, FM, FF], F32R)
        w2 = sb("w2", [P, FM, P], F32R)
        s_raw = sb("s_raw", [P, 3])
        s_pos, s_neg, s_sgn, s_sgn2, s_nsgn, s_abs = (
            sb(f"s_{n}", [P, 3]) for n in ("pos", "neg", "sgn", "sgn2", "nsgn", "abs"))
        s_01, s_01x4, s_fin = (sb(f"s_{n}", [P, 1]) for n in ("01", "01x4", "fin"))
        ident = sb("ident", [P, P])
        ones = sb("ones", [P, P])
        minus_half = sb("minus_half", [P, TILES])

        score_ps = [bank(f"score_ps{n}") for n in range(2)]
        turned_ps = [bank(f"turned_ps{n}") for n in range(2)]
        ffn_ps = [bank(f"ffn_ps{n}") for n in range(2)]
        misc_ps = [bank(f"misc_ps{n}") for n in range(2)]

        in_w = sem("in_w")
        in_b = sem("in_b")
        in_k = sem("in_k")
        in_s = sem("in_s")
        ones_made = sem("ones_made")
        ident_made = sem("ident_made")
        half_made = sem("half_made")
        k_zeroed = sem("k_zeroed")
        q_zeroed = sem("q_zeroed")
        v_zeroed = sem("v_zeroed")
        v_ones = sem("v_ones")
        scale_step = sem("scale_step")
        w_turned = sem("w_turned")
        w_kept = sem("w_kept")
        bv_made = sem("bv_made")
        bo_made = sem("bo_made")
        bo_kept = sem("bo_kept")
        ffn_w_made = sem("ffn_w_made")
        x_in = [sem(f"x_in{n}") for n in range(len(LOADS))]
        ctx_loaded = [sem(f"ctx_loaded{n}") for n in range(len(LOADS))]
        out_done = sem("out_done")
        q_written, k_written = sem("q_written"), sem("k_written")
        stacks_in = [sem(f"stacks_in{n}") for n in range(2)]
        st1_done, mv1_done, ve1_done, rs1_done, xn_done = (
            sem(n) for n in ("st1_done", "mv1_done", "ve1_done", "rs1_done", "xn_done"))
        x_biased = sem("x_biased")
        front_turned, qk_made, qk_hi, v_made = (
            sem(n) for n in ("front_turned", "qk_made", "qk_hi", "v_made"))
        scores_made, max_made, shift_done, scores_turned, exp_done = (
            sem(n) for n in ("scores_made", "max_made", "shift_done", "scores_turned", "exp_done"))
        pv_made, den_done, attn_turned, wo_made = (
            sem(n) for n in ("pv_made", "den_done", "attn_turned", "wo_made"))
        st2_done, mv2_done, ve2_done, rs2_done, xn2_done = (
            sem(n) for n in ("st2_done", "mv2_done", "ve2_done", "rs2_done", "xn2_done"))
        xn2_turned, xn2_hi = sem("xn2_turned"), sem("xn2_hi")
        ffn_made, ffn_hi, ffn_lo = sem("ffn_made"), sem("ffn_hi"), sem("ffn_lo")
        yt_made, y_made = sem("yt_made"), sem("y_made")
        misc_free = [sem(f"misc_free{n}") for n in range(2)]

        block = stack.enter_context(nc.Block())

        def tile(c, t, n=1):
            return slice(c * TILES + t, c * TILES + t + n)

        def misc_of(name):
            return misc_ps[misc_lag_bank(name)[1]]

        def free_misc(name):
            return misc_free[misc_lag_bank(name)[1]]

        def kept(eng, name, c):
            eng.wait_ge(free_misc(name), misc_used(name, c) + 1)

        def wait_load(eng, sems, c):
            for n, (first, _, _) in enumerate(LOADS):
                if first == c:
                    eng.wait_ge(sems[n], 16)

        def normalise(eng, c, dst, mv, rs, rs_done, done, free):
            eng.wait_ge(rs_done, c + 1)
            wait(eng, free, c)
            for t in range(TILES):
                op = eng.tensor_scalar(dst[:, t, :], x_all[:, c * TILES + t, :], mv[:, t, 0:1], rs[:, t:t + 1], ALU.subtract, ALU.mult)
            op.then_inc(done, 1)

        @block.sync
        def _(sp):
            def load(n):
                first, end, _ = LOADS[n]
                rows = slice(first * TILES, end * TILES)
                sp.dma_start(x_all[:, rows, :], x_v[:, rows, :]).then_inc(x_in[n], 16)
                sp.dma_start(ctx_all[:, rows, :], ctx_v[:, rows, :]).then_inc(ctx_loaded[n], 16)

            load(0)
            for n, w in enumerate((w_q, w_k, w_v, w_o)):
                sp.dma_start(w_nat[:, n, :], w).then_inc(in_w, 16)
            for col, b in ((bq_c, b_q), (bk_c, b_k)):
                sp.dma_start(col[:], b.rearrange("(g h d e) -> h d g e", g=G, h=4, e=1),
                             allow_slow_non_contiguous=True).then_inc(in_b, 16)
            sp.dma_start(bv_c[:], b_v.rearrange("(p e) -> p e", e=1)).then_inc(in_b, 16)
            sp.dma_start(bo_row[:], b_o.partition_broadcast(P)).then_inc(in_b, 16)

            def load_ffn_weights():
                sp.dma_start(k0_sb[:], k0.rearrange("(c p) n -> p c n", p=P)).then_inc(in_k, 16)
                sp.dma_start(k1_sb[:], k1.rearrange("(c p) n -> p c n", p=P)).then_inc(in_k, 16)
                sp.dma_start(k2_sb[:], k2.rearrange("(c p) n -> p c n", p=P)).then_inc(in_k, 16)
                for n, s in enumerate((s0, s1, s2)):
                    sp.dma_start(s_raw[:, n:n + 1], s.partition_broadcast(P)).then_inc(in_s, 16)

            load(1)
            load_ffn_weights()

            def write_parts(c, n):
                for v in range(2):
                    for u in range(2):
                        sp.dma_start(q_scr[n, :, v, u], parts[:, 0, v, :].bitcast(F32)).then_inc(q_written, 16)
                for u in range(2):
                    sp.dma_start(k_scr[n, :, u], parts[:, 1, u, :].bitcast(F32)).then_inc(k_written, 16)

            def load_stacks(c, n):
                sp.dma_start(q_st[n][:].bitcast(F32).rearrange("p g b q -> p (g b) q")[:, :, 0:SEQ],
                             q_scr[n].rearrange("h v u (d g) (b q) -> (h v u d) (g b) q", g=G, b=NB)).then_inc(stacks_in[n], 16)
                for h4 in range(4):
                    src = k_scr[n, h4].rearrange("u (d g) t -> (u d) g t", g=G).unsqueeze(0).broadcast_to([2, 2 * DH, G, CH])
                    sp.dma_start(k_st[n][32 * h4:32 * h4 + 32, :, h4, :].bitcast(F32), src).then_inc(stacks_in[n], 16)

            for i in range(turns):
                if live(i):
                    n = i % 2
                    kept(sp, "qk", i)
                    wait(sp, stacks_in[n], 80 * (i // 2))
                    write_parts(i, n)
                    if i < 2:
                        sp.wait_ge(q_zeroed, i + 1)
                        sp.wait_ge(k_zeroed, i + 1)
                    wait(sp, scores_made, UNITS * (i - 1))
                    sp.wait_ge(q_written, 64 * (i + 1))
                    sp.wait_ge(k_written, 32 * (i + 1))
                    load_stacks(i, n)
                for n, (_, _, turn) in enumerate(LOADS):
                    if turn == i:
                        load(n)
                if live(i - 4):
                    c = i - 4
                    kept(sp, "y", c)
                    sp.dma_start(out_v[:, tile(c, 0, TILES), :], x_all[:, tile(c, 0, TILES), :]).then_inc(out_done, 16)
            sp.wait_ge(out_done, 16 * chunks)

        @block.tensor
        def _(pe):
            def misc(name, c):
                wait(pe, free_misc(name), misc_used(name, c))
                return misc_of(name)

            def turn(o, col, src, n=TILES):
                for t in range(n):
                    mm = pe.transpose(o[:, col + t * P:col + (t + 1) * P], src[:, t, :], ident[:])
                return mm

            def scores(c, u):
                p, e = divmod(u, 2)
                n = c % 2
                if u == 0:
                    pe.wait_ge(stacks_in[n], 80 * (c // 2 + 1))
                wait(pe, shift_done, UNITS * c + u - 1)
                for j in range(2):
                    g = 2 * e + j
                    q = q_st[n][:].rearrange("p g b q -> p (g b q)")
                    for b in range(2):
                        first = (g * NB + 2 * p) * 2 * SEQ + b * SEQ
                        mm = pe.matmul(score_ps[u % 2][:, j * 4 * SEQ:(j + 1) * 4 * SEQ].rearrange("p (h k) -> p h k", h=4),
                                       q[:, first:first + 2 * SEQ], k_st[n][:, g, :, (2 * p + b) * SEQ:(2 * p + b + 1) * SEQ],
                                       start=(b == 0), stop=(b == 1))
                mm.then_inc(scores_made, 1)

            def turn_scores(c, u):
                pe.wait_ge(shift_done, UNITS * c + u + 1)
                wait(pe, exp_done, UNITS * c + u - 1)
                turn(turned_ps[u % 2], 0, shifted[u % 2][:].rearrange("p (a k) -> p a k", k=P), UH // 2).then_inc(scores_turned, 1)

            def values(c, p):
                pe.wait_ge(exp_done, UNITS * c + 2 * p + 2)
                if p == 0:
                    kept(pe, "v", c)
                o = misc(f"pv{p}", c)
                for hp in range(HP):
                    mm = pe.matmul(o[:, hp * OC:(hp + 1) * OC].rearrange("p (b c) -> p b c", b=2),
                                   probs[2 * p + hp // 4][:, hp % 4, :], v_bd[c % 2][:, 2 * p:2 * p + 2, hp, :], start=True, stop=True)
                mm.then_inc(pv_made, 1)

            def turn_attn(c, p):
                kept(pe, f"pv{p}", c)
                o = misc(f"out_t{p}", c)
                pe.transpose(o[:, 0:P], attn[p][:].rearrange("p a b d -> p (a b d)"), ident[:]).then_inc(attn_turned, 1)

            def project_out(c):
                kept(pe, "out_t0", c)
                kept(pe, "out_t1", c)
                o = misc("wo", c)
                for t in range(TILES):
                    mm = pe.matmul(o[:, t * P:(t + 1) * P], attn_t[:, t * P:(t + 1) * P], wo_t[:], start=True, stop=True)
                mm.then_inc(wo_made, 1)

            def turn_front(c):
                pe.wait_ge(xn_done, c + 1)
                wait_load(pe, ctx_loaded, c)
                o = misc("front_t", c)
                turn(o, 0, xn)
                turn(o, CH, ctx_all[:, tile(c, 0, TILES), :]).then_inc(front_turned, 1)

            def project_qk(c):
                kept(pe, "front_t", c)
                if c == 0:
                    pe.wait_ge(w_kept, 4)
                o = misc("qk", c)
                pe.matmul(o[:, 0:CH], wq_t[:], front[:, 0, :], start=True, stop=True)
                pe.matmul(o[:, CH:2 * CH], wk_t[:], front[:, 1, :], start=True, stop=True).then_inc(qk_made, 1)

            def project_v(c):
                o = misc("v", c)
                w = wv_t[:].rearrange("m (a b d) -> m b a d", b=2, d=DH)
                for n in range(NB):
                    keys = front[:, 1, n * SEQ:(n + 1) * SEQ]
                    for r in range(2):
                        mm = pe.matmul(o[r * SEQ:(r + 1) * SEQ, n * SEQ:(n + 1) * SEQ].rearrange("p (a d) -> p a d", d=DH),
                                       keys, w[:, r], start=True, stop=True)
                mm.then_inc(v_made, 1)

            def layer0(c, f):
                if f == 0:
                    kept(pe, "xn2_t", c)
                    if c == 0:
                        pe.wait_ge(ffn_w_made, 1)
                        pe.wait_ge(bo_kept, 1)
                wait(pe, ffn_lo, FT * c + f - 1)
                for j in range(2):
                    m = 2 * f + j
                    for part in range(2):
                        mm = pe.matmul(ffn_ps[f % 2][:, j * CH:(j + 1) * CH], w0[:, m * P:(m + 1) * P], xn2_t[:, part, :],
                                       start=(part == 0), stop=(part == 1))
                mm.then_inc(ffn_made, 1)

            def layer1(c, f):
                wait(pe, ffn_lo, FT * c + f - 1)
                for j in range(2):
                    m = 2 * (f - 2) + j
                    for k in range(FM):
                        if f == 2 and j == 0 and k == 2:
                            pe.wait_ge(ffn_lo, FT * c + 2)
                        for part in range(2):
                            mm = pe.matmul(ffn_ps[f % 2][:, j * CH:(j + 1) * CH], w1[:, k, m * P:(m + 1) * P], h1[:, part, k, :],
                                           start=(k == 0 and part == 0), stop=(k == FM - 1 and part == 1))
                mm.then_inc(ffn_made, 1)

            def layer2(c):
                pe.wait_ge(ffn_lo, FT * (c + 1))
                o = misc("y_t", c)
                for k in range(FM):
                    for part in range(2):
                        mm = pe.matmul(o[:, 0:CH], w2[:, k, :], h2[:, part, k, :],
                                       start=(k == 0 and part == 0), stop=(k == FM - 1 and part == 1))
                mm.then_inc(yt_made, 1)

            pe.wait_ge(ident_made, 1)
            pe.wait_ge(in_w, 64)
            turn(ffn_ps[0], 0, w_nat, 4).then_inc(w_turned, 1)

            for i in range(turns):
                if live(i - 2):
                    scores(i - 2, 2)
                    turn_scores(i - 2, 1)
                if live(i):
                    turn_front(i)
                if live(i - 3):
                    turn_attn(i - 3, 1)
                if live(i - 4):
                    layer1(i - 4, 2)
                if live(i - 3):
                    project_out(i - 3)
                if live(i):
                    project_qk(i)
                if live(i - 2):
                    scores(i - 2, 3)
                    turn_scores(i - 2, 2)
                    values(i - 2, 0)
                if live(i - 4):
                    layer1(i - 4, 3)
                if live(i - 1):
                    scores(i - 1, 0)
                if live(i - 2):
                    turn_scores(i - 2, 3)
                    turn_attn(i - 2, 0)
                if i == 0:
                    pe.wait_ge(bv_made, 1)
                    pe.matmul(ffn_ps[1][:, 0:P], bv_rep[:], wo_t[:], start=True, stop=True).then_inc(bo_made, 1)
                if live(i - 3):
                    pe.wait_ge(xn2_done, i - 2)
                    turn(misc("xn2_t", i - 3), 0, xn2).then_inc(xn2_turned, 1)
                if live(i - 4):
                    layer2(i - 4)
                if live(i - 1):
                    scores(i - 1, 1)
                    turn_scores(i - 1, 0)
                if live(i - 4):
                    kept(pe, "y_t", i - 4)
                    turn(misc("y", i - 4), 0, y_t[:].rearrange("p (t d) -> p t d", d=P)).then_inc(y_made, 1)
                if live(i - 2):
                    values(i - 2, 1)
                if live(i):
                    project_v(i)
                if live(i - 3):
                    layer0(i - 3, 0)
                    layer0(i - 3, 1)

        @block.scalar
        def _(act):
            def hi_ffn(c, f):
                h = h1 if f < 2 else h2
                act.wait_ge(ffn_made, FT * c + f + 1)
                m = 2 * (f % 2)
                act.activation(h[:, 0, m:m + 2, :], ffn_ps[f % 2][:].rearrange("p (m t) -> p m t", m=2), ACT.Relu).then_inc(ffn_hi, 1)

            def exp(c, u):
                act.wait_ge(scores_turned, UNITS * c + u + 1)
                wait(act, pv_made, TILES * (c - 1) + u // 2 + 1)
                act.activation(probs[u][:].rearrange("p a q -> p (a q)"), turned_ps[u % 2][:], ACT.Exp, scale=SCALE).then_inc(exp_done, 1)

            def keep_v(c):
                act.wait_ge(v_made, c + 1)
                wait(act, pv_made, TILES * (c - 1))
                if c == 0:
                    act.wait_ge(v_ones, 1)
                src = misc_of("v")[:, 0:NB * SEQ].rearrange("p (b a d) -> p b a d", b=NB, d=DH)
                for r in range(2):
                    rows = slice(r * SEQ, (r + 1) * SEQ)
                    cp = act.copy(v_bd[c % 2][rows, :, :, r * VC:r * VC + DH], src[rows])
                cp.then_inc(free_misc("v"), 1)

            def keep_attn_t(c, p):
                act.wait_ge(attn_turned, TILES * c + p + 1)
                if p == 0:
                    wait(act, wo_made, c)
                act.copy(attn_t[:, p * P:(p + 1) * P], misc_of(f"out_t{p}")[:, 0:P]).then_inc(free_misc(f"out_t{p}"), 1)

            def keep_front(c):
                act.wait_ge(front_turned, c + 1)
                wait(act, v_made, c)
                act.copy(front[:].rearrange("p a t -> p (a t)"), misc_of("front_t")[:]).then_inc(free_misc("front_t"), 1)

            def hi_qk(c):
                act.wait_ge(qk_made, c + 1)
                wait(act, q_written, 64 * c)
                wait(act, k_written, 32 * c)
                if c == 0:
                    act.wait_ge(in_b, 64)
                for n, bias in enumerate((bq_c, bk_c)):
                    op = act.activation(parts[:, n, 0, :], misc_of("qk")[:, n * CH:(n + 1) * CH], ACT.Identity, bias=bias[:, 0:1])
                op.then_inc(qk_hi, 1)

            act.wait_ge(w_turned, 1)
            for n, w in enumerate((wq_t, wk_t)):
                act.copy(w[:].rearrange("p (h d g) -> p g h d", h=4, g=G),
                         ffn_ps[0][:, n * P:(n + 1) * P].rearrange("p (g h d) -> p g h d", g=G, h=4)).then_inc(w_kept, 1)
            for n, w in enumerate((wv_t, wo_t)):
                act.copy(w[:], ffn_ps[0][:, (n + 2) * P:(n + 3) * P]).then_inc(w_kept, 1)

            for i in range(turns):
                if live(i - 2):
                    exp(i - 2, 1)
                if live(i):
                    keep_front(i)
                if live(i - 3):
                    keep_attn_t(i - 3, 1)
                if live(i - 4):
                    hi_ffn(i - 4, 2)
                if live(i):
                    hi_qk(i)
                if live(i - 2):
                    exp(i - 2, 2)
                if live(i - 4):
                    hi_ffn(i - 4, 3)
                if live(i - 2):
                    exp(i - 2, 3)
                    keep_attn_t(i - 2, 0)
                if live(i - 3):
                    act.wait_ge(xn2_turned, i - 2)
                    act.copy(xn2_t[:, 0, :], misc_of("xn2_t")[:, 0:CH]).then_inc(xn2_hi, 1)
                if live(i - 4):
                    act.wait_ge(yt_made, i - 3)
                    act.copy(y_t[:], misc_of("y_t")[:, 0:CH]).then_inc(free_misc("y_t"), 1)
                if live(i - 1):
                    exp(i - 1, 0)
                if live(i):
                    keep_v(i)
                if live(i - 3):
                    hi_ffn(i - 3, 0)
                    hi_ffn(i - 3, 1)

        @block.gpsimd
        def _(pool):
            pool.memset(ones[:], 1.0).then_inc(ones_made, 1)
            pool.wait_ge(ones_made, 1)
            pool.affine_select(out=ident[:], in_=ones[:], compare_op=ALU.is_equal, fill=0.0, base=0,
                               pattern=[[-1, P]], channel_multiplier=1).then_inc(ident_made, 1)
            pool.memset(minus_half[:], -0.5).then_inc(half_made, 1)
            pool.wait_ge(half_made, 1)

            def rstd(c, ve, rs, ve_done, rs_done):
                pool.wait_ge(ve_done, c + 1)
                pool.tensor_tensor(rs[:], ve[:], minus_half[:], ALU.pow).then_inc(rs_done, 1)

            rstd(0, ve1, rs1, ve1_done, rs1_done)

            for n in range(2):
                pool.memset(k_st[n][:].bitcast(U32), 0).then_inc(k_zeroed, 1)

            for i in range(turns):
                if live(i + 1):
                    rstd(i + 1, ve1, rs1, ve1_done, rs1_done)
                if live(i - 3):
                    rstd(i - 3, ve2, rs2, ve2_done, rs2_done)
                if live(i + 1):
                    normalise(pool, i + 1, xn, mv1, rs1, rs1_done, xn_done, front_turned)
                if live(i):
                    if i == 0:
                        pool.wait_ge(bo_kept, 1)
                    pool.wait_ge(xn_done, i + 1)
                    xa = x_all[:, tile(i, 0, TILES), :]
                    pool.tensor_tensor(xa, xa, bo_row[:].unsqueeze(1).broadcast_to([P, TILES, P]), ALU.add).then_inc(x_biased, 1)

        @block.vector
        def _(dve):
            def stats(c, st, mv, ve, st_done, mv_done, ve_done):
                for t in range(TILES):
                    op = dve.bn_stats(st[:, t, :], x_all[:, c * TILES + t, :])
                op.then_inc(st_done, 1)
                dve.wait_ge(st_done, c + 1)
                for t in range(TILES):
                    op = dve.bn_aggr(mv[:, t, :], st[:, t, :])
                op.then_inc(mv_done, 1)
                dve.wait_ge(mv_done, c + 1)
                dve.tensor_scalar(ve[:], mv[:, :, 1], EPS, None, ALU.add).then_inc(ve_done, 1)

            def stats1(c):
                wait_load(dve, x_in, c)
                wait(dve, xn_done, c)
                stats(c, st1, mv1, ve1, st1_done, mv1_done, ve1_done)

            def shift(c, u):
                n = u % 2
                scores = score_ps[n][:].rearrange("p (a k) -> p a k", a=UH)
                dve.wait_ge(scores_made, UNITS * c + u + 1)
                dve.tensor_reduce(row_max[n][:], scores, AX.X, ALU.max).then_inc(max_made, 1)
                dve.wait_ge(max_made, UNITS * c + u + 1)
                wait(dve, scores_turned, UNITS * c + u - 1)
                dve.tensor_tensor(shifted[n][:].rearrange("p (a k) -> p a k", a=UH), scores,
                                  row_max[n][:].unsqueeze(2).broadcast_to([P, UH, SEQ]), ALU.subtract).then_inc(shift_done, 1)

            def lo_ffn(c, f):
                h = h1 if f < 2 else h2
                m = 2 * (f % 2)
                dve.wait_ge(ffn_hi, FT * c + f + 1)
                dve.scalar_tensor_tensor(out=h[:, 1, m:m + 2, :], in0=ffn_ps[f % 2][:].rearrange("p (m t) -> p m t", m=2), scalar=0.0,
                                         in1=h[:, 0, m:m + 2, :].bitcast(F32), op0=ALU.max, op1=ALU.subtract).then_inc(ffn_lo, 1)

            def lo_part(lo, hi, product, bias):
                return dve.scalar_tensor_tensor(out=lo, in0=product, scalar=bias, in1=hi.bitcast(F32), op0=ALU.add, op1=ALU.subtract)

            def normalise_attn(c, p):
                dve.wait_ge(pv_made, TILES * c + p + 1)
                wait(dve, attn_turned, TILES * (c - 1) + p + 1)
                o = misc_of(f"pv{p}")[:, 0:HP * OC].rearrange("p (a b r c) -> p b a r c", a=HP, b=2, r=2)
                for b in range(2):
                    rows = slice(b * SEQ, (b + 1) * SEQ)
                    op = dve.reciprocal(inv_den[p][rows], o[rows, b, :, :, DH])
                op.then_inc(den_done, 1)
                dve.wait_ge(den_done, TILES * c + p + 1)
                for b in range(2):
                    rows = slice(b * SEQ, (b + 1) * SEQ)
                    op = dve.tensor_tensor(attn[p][rows], o[rows, b, :, :, 0:DH],
                                           inv_den[p][rows].unsqueeze(3).broadcast_to([SEQ, HP, 2, DH]), ALU.mult)
                op.then_inc(free_misc(f"pv{p}"), 1)

            def add_attention(c):
                dve.wait_ge(wo_made, c + 1)
                dve.wait_ge(x_biased, c + 1)
                xa = x_all[:, tile(c, 0, TILES), :]
                dve.tensor_tensor(xa, misc_of("wo")[:, 0:CH].rearrange("p (t d) -> p t d", t=TILES), xa, ALU.add).then_inc(free_misc("wo"), 1)
                kept(dve, "wo", c)
                stats(c, st2, mv2, ve2, st2_done, mv2_done, ve2_done)

            def lo_qk(c):
                dve.wait_ge(qk_hi, c + 1)
                for n, bias in enumerate((bq_c, bk_c)):
                    op = lo_part(parts[:, n, 1, :], parts[:, n, 0, :], misc_of("qk")[:, n * CH:(n + 1) * CH], bias[:, 0:1])
                op.then_inc(free_misc("qk"), 1)

            stats1(0)
            normalise(dve, 0, xn, mv1, rs1, rs1_done, xn_done, front_turned)
            for n in range(2):
                dve.memset(q_st[n][:].bitcast(U32), 0).then_inc(q_zeroed, 1)
            for n in range(2):
                dve.memset(v_bd[n][:], 0.0).then_inc(v_zeroed, 1)
            dve.wait_ge(v_zeroed, 2)
            for n in range(2):
                for r in range(2):
                    op = dve.memset(v_bd[n][r * SEQ:(r + 1) * SEQ, :, :, r * VC + DH:r * VC + DH + 1], 1.0)
            op.then_inc(v_ones, 1)
            dve.wait_ge(in_b, 64)
            dve.wait_ge(ones_made, 1)
            dve.tensor_scalar(bv_rep[:], ones[:], bv_c[:, 0:1], None, ALU.mult).then_inc(bv_made, 1)

            def setup_ffn():
                dve.wait_ge(in_s, 48)
                dve.wait_ge(in_k, 48)
                dve.tensor_scalar(s_pos[:], s_raw[:], 0.0, None, ALU.is_gt)
                dve.tensor_scalar(s_neg[:], s_raw[:], 0.0, None, ALU.is_lt).then_inc(scale_step, 1)
                dve.wait_ge(scale_step, 1)
                dve.tensor_tensor(s_sgn[:], s_pos[:], s_neg[:], ALU.subtract)
                dve.tensor_tensor(k0_diff[:], k0_sb[:, 0, :], k0_sb[:, 1, :], ALU.subtract).then_inc(scale_step, 1)
                dve.wait_ge(scale_step, 2)
                dve.tensor_scalar(s_sgn2[:], s_sgn[:], 2.0, None, ALU.mult)
                dve.tensor_scalar(s_nsgn[:], s_sgn[:], -1.0, None, ALU.mult)
                dve.tensor_tensor(s_abs[:], s_raw[:], s_sgn[:], ALU.mult).then_inc(scale_step, 1)
                dve.wait_ge(scale_step, 3)
                dve.tensor_scalar(w0[:], k0_diff[:], s_sgn2[:, 0:1], None, ALU.mult)
                dve.tensor_scalar(w1[:], k1_sb[:], s_sgn2[:, 1:2], s_nsgn[:, 1:2], ALU.mult, ALU.add)
                dve.tensor_scalar(w2[:], k2_sb[:], 2.0, -1.0, ALU.mult, ALU.add)
                dve.tensor_tensor(s_01[:], s_abs[:, 0:1], s_abs[:, 1:2], ALU.mult).then_inc(scale_step, 1)
                dve.wait_ge(scale_step, 4)
                dve.tensor_scalar(s_01x4[:], s_01[:], 4.0, None, ALU.mult).then_inc(scale_step, 1)
                dve.wait_ge(scale_step, 5)
                dve.tensor_tensor(s_fin[:], s_01x4[:], s_raw[:, 2:3], ALU.mult).then_inc(ffn_w_made, 1)
                dve.wait_ge(ffn_w_made, 1)

            for i in range(turns):
                if live(i - 2):
                    shift(i - 2, 2)
                if live(i + 1):
                    stats1(i + 1)
                if live(i - 3):
                    add_attention(i - 3)
                if live(i - 4):
                    lo_ffn(i - 4, 2)
                if live(i):
                    lo_qk(i)
                if live(i - 2):
                    shift(i - 2, 3)
                if live(i - 3):
                    normalise(dve, i - 3, xn2, mv2, rs2, rs2_done, xn2_done, xn2_turned)
                if live(i - 2):
                    normalise_attn(i - 2, 0)
                if live(i - 4):
                    lo_ffn(i - 4, 3)
                if live(i - 1):
                    shift(i - 1, 0)
                if i == 0:
                    dve.wait_ge(bo_made, 1)
                    dve.tensor_tensor(bo_row[:], ffn_ps[1][:, 0:P], bo_row[:], ALU.add).then_inc(bo_kept, 1)
                    setup_ffn()
                if live(i - 3):
                    dve.wait_ge(xn2_hi, i - 2)
                    lo_part(xn2_t[:, 1, :], xn2_t[:, 0, :], misc_of("xn2_t")[:, 0:CH], 0.0).then_inc(free_misc("xn2_t"), 1)
                if live(i - 1):
                    shift(i - 1, 1)
                if live(i - 4):
                    dve.wait_ge(y_made, i - 3)
                    xa = x_all[:, tile(i - 4, 0, TILES), :]
                    dve.scalar_tensor_tensor(out=xa, in0=misc_of("y")[:, 0:CH].rearrange("p (t d) -> p t d", t=TILES), scalar=s_fin[:, 0:1], in1=xa,
                                             op0=ALU.mult, op1=ALU.add).then_inc(free_misc("y"), 1)
                if live(i - 2):
                    normalise_attn(i - 2, 1)
                if live(i - 3):
                    lo_ffn(i - 3, 0)
                    lo_ffn(i - 3, 1)
    return nc


_INS = ['x', 'ctx_1024', 'L0_xattn_w_q', 'L0_xattn_b_q', 'L0_xattn_w_k', 'L0_xattn_b_k', 'L0_xattn_w_v', 'L0_xattn_b_v',
        'L0_xattn_w_o', 'L0_xattn_b_o', 'L0_ffn_k0', 'L0_ffn_k1', 'L0_ffn_k2', 'L0_ffn_s0', 'L0_ffn_s1', 'L0_ffn_s2']


def kernel(**inputs):
    import numpy as _np
    import concourse.bacc as _bacc
    from concourse import mybir as _mybir
    from concourse.bass_utils import run_bass_kernel_spmd as _run

    nc = _bacc.Bacc("TRN2", target_bir_lowering=False, num_devices=1)
    arrays, args = {}, []
    for name in _INS:
        a = _np.ascontiguousarray(inputs[name])
        if a.ndim == 0:
            a = a.reshape(1)
        arrays[f"in_{name}_dram"] = a
        args.append(nc.dram_tensor(f"in_{name}_dram", a.shape, _mybir.dt.from_np(a.dtype), kind="ExternalInput").ap())
    shape = tuple(_np.shape(inputs['x']))
    args.append(nc.dram_tensor("out_0_dram", shape, _mybir.dt.float32, kind="ExternalOutput").ap())
    program(nc, *args)
    r = _run(nc, [arrays], core_ids=[0])
    return r.results[0]["out_0_dram"]
```

```python
from contextlib import ExitStack

import concourse.bass as bass
from concourse import mybir

F32 = mybir.dt.float32
F32R = mybir.dt.float32r
U8 = mybir.dt.uint8
U32 = mybir.dt.uint32
ALU = mybir.AluOpType
ACT = mybir.ActivationFunctionType
AX = mybir.AxisListType

P = 128
SEQ = 64
HEADS = 16
DH = P // HEADS
HP = HEADS // 2
G = 4
NB = 4
CH = NB * SEQ
TILES = CH // P
UNITS = 2 * TILES
UH = HEADS // 2
SLOTS = UNITS
FF = 512
FM = FF // P
FT = 2 * FM // 2
FLO = FT - 1
VC = DH + 1
OC = 2 * 2 * VC
EPS = 1e-5
SCALE = float(DH) ** -0.5
LAG = 4

DMA = 16
Q_WRITES = 2 * 2 * DMA
K_WRITES = 2 * DMA
STACK_LOADS = 5 * DMA

MISC = [
    ("out_t1", 3, 1), ("front_t", 0, 0), ("wo", 3, 1), ("qk", 0, 0), ("pv0", 2, 1), ("v", 1, 0),
    ("out_t0", 2, 1), ("xn2_t", 3, 0), ("y_t", 4, 1), ("pv1", 2, 0), ("y", 4, 1),
]
LOADS = [(0, 1, None), (1, 4, None), (4, 8, 1), (8, None, 2)]


def program(nc, x, ctx_in, w_q, b_q, w_k, b_k, w_v, b_v, w_o, b_o, k0, k1, k2, s0, s1, s2, out):
    chunks = x.shape[0] * x.shape[1] // CH
    turns = chunks + LAG
    x_v = x.rearrange("b s d -> (b s) d").rearrange("(t p) d -> p t d", p=P)
    ctx_v = ctx_in.rearrange("b s d -> (b s) d").rearrange("(t p) d -> p t d", p=P)
    out_v = out.rearrange("b s d -> (b s) d").rearrange("(t p) d -> p t d", p=P)
    q_scr = nc.dram_tensor("q_scr", [2, G, 2, 2, DH * G, CH], F32, kind="Internal").ap()
    k_scr = nc.dram_tensor("k_scr", [2, G, 2, DH * G, CH], F32, kind="Internal").ap()

    def live(c):
        return 0 <= c < chunks

    def misc_lag_bank(name):
        return next((lag, b) for n, lag, b in MISC if n == name)

    def misc_used(name, c):
        lag, bank_no = misc_lag_bank(name)
        turn, place = c + lag, [n for n, _, _ in MISC].index(name)
        return sum(live(t - l) for t in range(turn + 1) for m, (_, l, b) in enumerate(MISC)
                   if b == bank_no and (t < turn or m < place))

    def wait(eng, sem, value):
        if value > 0:
            eng.wait_ge(sem, value)

    with ExitStack() as stack:
        def sb(name, shape, dt=F32):
            return stack.enter_context(nc.sbuf_tensor(name, shape, dt))

        def bank(name):
            return stack.enter_context(nc.psum_tensor(name, [P, 512], F32))

        def sem(name):
            return stack.enter_context(nc.semaphore(name))

        x_all = sb("x_all", [P, chunks * TILES, P])
        ctx_all = sb("ctx_all", [P, chunks * TILES, P])
        xn = sb("xn", [P, TILES, P])
        front = [sb(f"front{n}", [P, 2, CH]) for n in range(2)]
        qk_full = sb("qk_full", [P, 2, CH])
        parts = sb("parts", [P, 2, 2, CH], F32R)
        q_st = [sb(f"q_st{n}", [P, G, TILES, 4, SEQ], F32R) for n in range(2)]
        k_st = [sb(f"k_st{n}", [P, G, 4, CH], F32R) for n in range(2)]
        v_bd = [sb(f"v_bd{n}", [P, NB, HP, 2 * VC]) for n in range(2)]
        row_max = [sb(f"row_max{n}", [P, UH]) for n in range(2)]
        shifted = [sb(f"shifted{n}", [P, UH * SEQ]) for n in range(2)]
        probs = [sb(f"probs{n}", [P, UH // 2, P]) for n in range(UNITS)]
        inv_den = [sb(f"inv_den{n}", [P, HP, 2]) for n in range(TILES)]
        attn = [sb(f"attn{n}", [P, HP, 2, DH]) for n in range(TILES)]
        attn_t = sb("attn_t", [P, CH])
        xn2 = sb("xn2", [P, TILES, P])
        xn2_t = sb("xn2_t", [P, 2, CH], F32R)
        h1 = sb("h1", [P, 2, FM, CH], F32R)
        h2 = sb("h2", [P, 2, FM, CH], F32R)
        h2_full = sb("h2_full", [P, 2, CH])
        y_t = sb("y_t", [P, CH])
        st1, st2 = (sb(f"st{n}", [P, TILES, 6]) for n in (1, 2))
        mv1, mv2 = (sb(f"mv{n}", [P, TILES, 2]) for n in (1, 2))
        ve1, ve2 = (sb(f"ve{n}", [P, TILES]) for n in (1, 2))
        rs1, rs2 = (sb(f"rs{n}", [P, TILES]) for n in (1, 2))
        w_nat = sb("w_nat", [P, 4, P])
        wq_t, wk_t, wv_t, wo_t = (sb(f"{n}_t", [P, P]) for n in ("wq", "wk", "wv", "wo"))
        bq_c, bk_c, bv_c = (sb(f"b{n}_c", [P, 1]) for n in "qkv")
        bo_row = sb("bo_row", [P, P])
        bv_rep = sb("bv_rep", [P, P])
        k0_sb = sb("k0_sb", [P, 2, FF], U8)
        k1_sb = sb("k1_sb", [P, FM, FF], U8)
        k2_sb = sb("k2_sb", [P, FM, P], U8)
        k0_diff = sb("k0_diff", [P, FF])
        w0 = sb("w0", [P, FF], F32R)
        w1 = sb("w1", [P, FM, FF], F32R)
        w2 = sb("w2", [P, FM, P], F32R)
        s_raw = sb("s_raw", [P, 3])
        s_pos, s_neg, s_sgn, s_sgn2, s_nsgn, s_abs = (
            sb(f"s_{n}", [P, 3]) for n in ("pos", "neg", "sgn", "sgn2", "nsgn", "abs"))
        s_01, s_01x4, s_fin = (sb(f"s_{n}", [P, 1]) for n in ("01", "01x4", "fin"))
        ident = sb("ident", [P, P])
        ones = sb("ones", [P, P])
        minus_half = sb("minus_half", [P, TILES])

        score_ps = [bank(f"score_ps{n}") for n in range(2)]
        turned_ps = [bank(f"turned_ps{n}") for n in range(2)]
        ffn_ps = [bank(f"ffn_ps{n}") for n in range(2)]
        misc_ps = [bank(f"misc_ps{n}") for n in range(2)]

        in_w = sem("in_w")
        in_b = sem("in_b")
        in_k = sem("in_k")
        in_s = sem("in_s")
        ones_made = sem("ones_made")
        ident_made = sem("ident_made")
        half_made = sem("half_made")
        k_zeroed = sem("k_zeroed")
        q_zeroed = sem("q_zeroed")
        v_zeroed = sem("v_zeroed")
        v_ones = sem("v_ones")
        scale_step = sem("scale_step")
        w_turned = sem("w_turned")
        w_kept = sem("w_kept")
        bv_made = sem("bv_made")
        bo_made = sem("bo_made")
        bo_kept = sem("bo_kept")
        ffn_w_made = sem("ffn_w_made")
        x_in = [sem(f"x_in{n}") for n in range(len(LOADS))]
        ctx_loaded = [sem(f"ctx_loaded{n}") for n in range(len(LOADS))]
        out_done = sem("out_done")
        q_written, k_written = sem("q_written"), sem("k_written")
        stacks_in = [sem(f"stacks_in{n}") for n in range(2)]
        st1_done, mv1_done, ve1_done, rs1_done, xn_done = (
            sem(n) for n in ("st1_done", "mv1_done", "ve1_done", "rs1_done", "xn_done"))
        x_biased = sem("x_biased")
        front_turned, qk_made, qk_hi, qk_lo, v_made = (
            sem(n) for n in ("front_turned", "qk_made", "qk_hi", "qk_lo", "v_made"))
        scores_made, max_made, shift_done, scores_turned, exp_done = (
            sem(n) for n in ("scores_made", "max_made", "shift_done", "scores_turned", "exp_done"))
        pv_made, den_done, attn_turned, wo_made = (
            sem(n) for n in ("pv_made", "den_done", "attn_turned", "wo_made"))
        st2_done, mv2_done, ve2_done, rs2_done, xn2_done = (
            sem(n) for n in ("st2_done", "mv2_done", "ve2_done", "rs2_done", "xn2_done"))
        xn2_turned, xn2_hi = sem("xn2_turned"), sem("xn2_hi")
        ffn_made, ffn_hi = sem("ffn_made"), sem("ffn_hi")
        ffn_lo = sem("ffn_lo")
        h2_kept = sem("h2_kept")
        h2_lo = sem("h2_lo")
        yt_made, y_made = sem("yt_made"), sem("y_made")
        misc_free = [sem(f"misc_free{n}") for n in range(2)]

        block = stack.enter_context(nc.Block())

        def tile(c, t, n=1):
            return slice(c * TILES + t, c * TILES + t + n)

        def misc_of(name):
            return misc_ps[misc_lag_bank(name)[1]]

        def free_misc(name):
            return misc_free[misc_lag_bank(name)[1]]

        def kept(eng, name, c):
            eng.wait_ge(free_misc(name), misc_used(name, c) + 1)

        def closing(i):
            return i - 3 == chunks - 1

        def wait_load(eng, sems, c):
            for n, (first, _, _) in enumerate(LOADS):
                if first == c:
                    eng.wait_ge(sems[n], DMA)

        def normalise(eng, c, dst, mv, rs, rs_done, done, free):
            eng.wait_ge(rs_done, c + 1)
            wait(eng, free, c)
            for t in range(TILES):
                op = eng.tensor_scalar(dst[:, t, :], x_all[:, c * TILES + t, :], mv[:, t, 0:1], rs[:, t:t + 1], ALU.subtract, ALU.mult)
            op.then_inc(done, 1)

        @block.sync
        def _(sp):
            def load(n):
                first, end, _ = LOADS[n]
                rows = slice(first * TILES, (end or chunks) * TILES)
                sp.dma_start(x_all[:, rows, :], x_v[:, rows, :]).then_inc(x_in[n], DMA)
                sp.dma_start(ctx_all[:, rows, :], ctx_v[:, rows, :]).then_inc(ctx_loaded[n], DMA)

            load(0)
            for n, w in enumerate((w_q, w_k, w_v, w_o)):
                sp.dma_start(w_nat[:, n, :], w).then_inc(in_w, DMA)
            for col, b in ((bq_c, b_q), (bk_c, b_k)):
                sp.dma_start(col[:], b.rearrange("(g h d e) -> h d g e", g=G, h=4, e=1),
                             allow_slow_non_contiguous=True).then_inc(in_b, DMA)
            sp.dma_start(bv_c[:], b_v.rearrange("(p e) -> p e", e=1)).then_inc(in_b, DMA)
            sp.dma_start(bo_row[:], b_o.partition_broadcast(P)).then_inc(in_b, DMA)

            def load_ffn_weights():
                sp.dma_start(k0_sb[:], k0.rearrange("(c p) n -> p c n", p=P)).then_inc(in_k, DMA)
                sp.dma_start(k1_sb[:], k1.rearrange("(c p) n -> p c n", p=P)).then_inc(in_k, DMA)
                sp.dma_start(k2_sb[:], k2.rearrange("(c p) n -> p c n", p=P)).then_inc(in_k, DMA)
                for n, s in enumerate((s0, s1, s2)):
                    sp.dma_start(s_raw[:, n:n + 1], s.partition_broadcast(P)).then_inc(in_s, DMA)

            load(1)
            load_ffn_weights()

            def write_parts(n, part):
                for u in range(2):
                    sp.dma_start(q_scr[n, :, part, u], parts[:, 0, part, :].bitcast(F32)).then_inc(q_written, DMA)
                sp.dma_start(k_scr[n, :, part], parts[:, 1, part, :].bitcast(F32)).then_inc(k_written, DMA)

            def load_stacks(n):
                sp.dma_start(q_st[n][:].bitcast(F32).rearrange("p g t b q -> p (g t) (b q)")[:, :, SEQ:3 * SEQ],
                             q_scr[n].rearrange("h v u (d g) (t q) -> (h v u d) (g t) q", g=G, t=TILES)).then_inc(stacks_in[n], DMA)
                for h4 in range(4):
                    src = k_scr[n, h4].rearrange("u (d g) t -> (u d) g t", g=G).unsqueeze(0).broadcast_to([2, 2 * DH, G, CH])
                    sp.dma_start(k_st[n][32 * h4:32 * h4 + 32, :, h4, :].bitcast(F32), src).then_inc(stacks_in[n], DMA)

            for i in range(turns):
                if live(i):
                    n = i % 2
                    wait(sp, stacks_in[n], STACK_LOADS * (i // 2))
                    sp.wait_ge(qk_hi, i + 1)
                    write_parts(n, 0)
                    sp.wait_ge(qk_lo, i + 1)
                    write_parts(n, 1)
                    if i < 2:
                        sp.wait_ge(q_zeroed, i + 1)
                        sp.wait_ge(k_zeroed, i + 1)
                    wait(sp, scores_made, UNITS * (i - 1))
                    sp.wait_ge(q_written, Q_WRITES * (i + 1))
                    sp.wait_ge(k_written, K_WRITES * (i + 1))
                    load_stacks(n)
                for n, (_, _, turn) in enumerate(LOADS):
                    if turn == i:
                        load(n)
                if live(i - 4):
                    c = i - 4
                    kept(sp, "y", c)
                    sp.dma_start(out_v[:, tile(c, 0, TILES), :], x_all[:, tile(c, 0, TILES), :]).then_inc(out_done, DMA)
            sp.wait_ge(out_done, DMA * chunks)

        @block.tensor
        def _(pe):
            def misc(name, c):
                wait(pe, free_misc(name), misc_used(name, c))
                return misc_of(name)

            def turn(o, col, src, n=TILES):
                for t in range(n):
                    mm = pe.transpose(o[:, col + t * P:col + (t + 1) * P], src[:, t, :], ident[:])
                return mm

            def scores(c, u):
                p, e = divmod(u, 2)
                n = c % 2
                if u == 0:
                    pe.wait_ge(stacks_in[n], STACK_LOADS * (c // 2 + 1))
                wait(pe, shift_done, UNITS * c + u - 1)
                for j in range(2):
                    g = 2 * e + j
                    q = q_st[n][:, g, p].rearrange("p b q -> p (b q)")
                    for b in range(2):
                        first = (1 - b) * 2 * SEQ
                        mm = pe.matmul(score_ps[u % 2][:, j * 4 * SEQ:(j + 1) * 4 * SEQ].rearrange("p (h k) -> p h k", h=4),
                                       q[:, first:first + 2 * SEQ], k_st[n][:, g, :, (2 * p + b) * SEQ:(2 * p + b + 1) * SEQ],
                                       start=(b == 0), stop=(b == 1))
                mm.then_inc(scores_made, 1)

            def turn_scores(c, u):
                pe.wait_ge(shift_done, UNITS * c + u + 1)
                wait(pe, exp_done, UNITS * c + u - 1)
                turn(turned_ps[u % 2], 0, shifted[u % 2][:].rearrange("p (a k) -> p a k", k=P), UH // 2).then_inc(scores_turned, 1)

            def values(c, p):
                pe.wait_ge(exp_done, UNITS * c + 2 * p + 2)
                if p == 0:
                    kept(pe, "v", c)
                o = misc(f"pv{p}", c)
                for hp in range(HP):
                    mm = pe.matmul(o[:, hp * OC:(hp + 1) * OC].rearrange("p (b c) -> p b c", b=2),
                                   probs[2 * p + hp // 4][:, hp % 4, :], v_bd[c % 2][:, 2 * p:2 * p + 2, hp, :], start=True, stop=True)
                mm.then_inc(pv_made, 1)

            def turn_attn(c, p):
                kept(pe, f"pv{p}", c)
                o = misc(f"out_t{p}", c)
                pe.transpose(o[:, 0:P], attn[p][:].rearrange("p a b d -> p (a b d)"), ident[:]).then_inc(attn_turned, 1)

            def project_out(c):
                kept(pe, "out_t0", c)
                kept(pe, "out_t1", c)
                o = misc("wo", c)
                for t in range(TILES):
                    mm = pe.matmul(o[:, t * P:(t + 1) * P], attn_t[:, t * P:(t + 1) * P], wo_t[:], start=True, stop=True)
                mm.then_inc(wo_made, 1)

            def turn_front(c):
                pe.wait_ge(xn_done, c + 1)
                wait_load(pe, ctx_loaded, c)
                o = misc("front_t", c)
                turn(o, 0, xn)
                turn(o, CH, ctx_all[:, tile(c, 0, TILES), :]).then_inc(front_turned, 1)

            def project_qk(c):
                kept(pe, "front_t", c)
                if c == 0:
                    pe.wait_ge(w_kept, 4)
                o = misc("qk", c)
                for b in range(2):
                    pe.matmul(o[:, 0:CH].rearrange("p (t b q) -> p b t q", b=2, q=SEQ)[:, 1 - b], wq_t[:],
                              front[c % 2][:, 0, :].rearrange("p (t b q) -> p b t q", b=2, q=SEQ)[:, b], start=True, stop=True)
                pe.matmul(o[:, CH:2 * CH], wk_t[:], front[c % 2][:, 1, :], start=True, stop=True).then_inc(qk_made, 1)

            def project_v(c):
                o = misc("v", c)
                w = wv_t[:].rearrange("m (a b d) -> m b a d", b=2, d=DH)
                for n in range(NB):
                    keys = front[c % 2][:, 1, n * SEQ:(n + 1) * SEQ]
                    for r in range(2):
                        mm = pe.matmul(o[r * SEQ:(r + 1) * SEQ, n * SEQ:(n + 1) * SEQ].rearrange("p (a d) -> p a d", d=DH),
                                       keys, w[:, r], start=True, stop=True)
                mm.then_inc(v_made, 1)

            def layer0(c, f):
                if f == 0:
                    kept(pe, "xn2_t", c)
                    if c == 0:
                        pe.wait_ge(ffn_w_made, 1)
                        pe.wait_ge(bo_kept, 1)
                    wait(pe, h2_kept, c)
                else:
                    wait(pe, ffn_lo, FLO * c)
                for j in range(2):
                    m = 2 * f + j
                    for part in range(2):
                        mm = pe.matmul(ffn_ps[f % 2][:, j * CH:(j + 1) * CH], w0[:, m * P:(m + 1) * P], xn2_t[:, part, :],
                                       start=(part == 0), stop=(part == 1))
                mm.then_inc(ffn_made, 1)

            def layer1(c, f):
                pe.wait_ge(ffn_lo, FLO * c + f - 1)
                for j in range(2):
                    m = 2 * (f - 2) + j
                    for k in range(FM):
                        if f == 2 and j == 0 and k == 2:
                            pe.wait_ge(ffn_lo, FLO * c + 2)
                        for part in range(2):
                            mm = pe.matmul(ffn_ps[f % 2][:, j * CH:(j + 1) * CH], w1[:, k, m * P:(m + 1) * P], h1[:, part, k, :],
                                           start=(k == 0 and part == 0), stop=(k == FM - 1 and part == 1))
                mm.then_inc(ffn_made, 1)

            def layer2(c):
                pe.wait_ge(h2_lo, c + 1)
                pe.wait_ge(ffn_lo, FLO * (c + 1))
                o = misc("y_t", c)
                for k in range(FM):
                    for part in range(2):
                        mm = pe.matmul(o[:, 0:CH], w2[:, k, :], h2[:, part, k, :],
                                       start=(k == 0 and part == 0), stop=(k == FM - 1 and part == 1))
                mm.then_inc(yt_made, 1)

            def keep_warm(times):
                for _ in range(times):
                    pe.transpose(turned_ps[1][:, 0:P], ident[:], ident[:])

            pe.wait_ge(ident_made, 1)
            keep_warm(18)
            pe.wait_ge(in_w, 4 * DMA)
            turn(ffn_ps[0], 0, w_nat, 4).then_inc(w_turned, 1)

            for i in range(turns):
                if live(i - 2):
                    scores(i - 2, 2)
                if live(i - 3):
                    turn_attn(i - 3, 1)
                if live(i - 2):
                    turn_scores(i - 2, 1)
                if live(i):
                    turn_front(i)
                if live(i - 3):
                    project_out(i - 3)
                if live(i - 4):
                    layer1(i - 4, 2)
                if live(i):
                    project_qk(i)
                if live(i - 2):
                    scores(i - 2, 3)
                    turn_scores(i - 2, 2)
                    values(i - 2, 0)
                if live(i - 4):
                    layer1(i - 4, 3)
                if i == 1:
                    keep_warm(16)
                if live(i - 1):
                    scores(i - 1, 0)
                    project_v(i - 1)
                if live(i - 2):
                    turn_attn(i - 2, 0)
                    turn_scores(i - 2, 3)
                if i == 0:
                    pe.wait_ge(bv_made, 1)
                    pe.matmul(ffn_ps[1][:, 0:P], bv_rep[:], wo_t[:], start=True, stop=True).then_inc(bo_made, 1)
                if live(i - 1):
                    scores(i - 1, 1)
                if live(i - 3):
                    pe.wait_ge(xn2_done, i - 2)
                    turn(misc("xn2_t", i - 3), 0, xn2).then_inc(xn2_turned, 1)
                if closing(i):
                    layer0(i - 3, 0)
                    layer0(i - 3, 1)
                if live(i - 4):
                    layer2(i - 4)
                if live(i - 1):
                    turn_scores(i - 1, 0)
                if live(i - 2):
                    values(i - 2, 1)
                if live(i - 3) and not closing(i):
                    layer0(i - 3, 0)
                if live(i - 4):
                    kept(pe, "y_t", i - 4)
                    turn(misc("y", i - 4), 0, y_t[:].rearrange("p (t d) -> p t d", d=P)).then_inc(y_made, 1)
                if live(i - 3) and not closing(i):
                    layer0(i - 3, 1)

        @block.scalar
        def _(act):
            def hi_ffn(c, f):
                h = h1 if f < 2 else h2
                act.wait_ge(ffn_made, FT * c + f + 1)
                m = 2 * (f % 2)
                act.activation(h[:, 0, m:m + 2, :], ffn_ps[f % 2][:].rearrange("p (m t) -> p m t", m=2), ACT.Relu).then_inc(ffn_hi, 1)
                if f == 2:
                    wait(act, h2_lo, c)
                    act.activation(h2_full[:].rearrange("p m t -> p (m t)"), ffn_ps[0][:], ACT.Relu).then_inc(h2_kept, 1)

            def exp(c, u):
                act.wait_ge(scores_turned, UNITS * c + u + 1)
                wait(act, pv_made, TILES * (c - 1) + u // 2 + 1)
                act.activation(probs[u][:].rearrange("p a q -> p (a q)"), turned_ps[u % 2][:], ACT.Exp, scale=SCALE).then_inc(exp_done, 1)

            def keep_v(c):
                act.wait_ge(v_made, c + 1)
                wait(act, pv_made, TILES * (c - 1))
                if c == 0:
                    act.wait_ge(v_ones, 1)
                src = misc_of("v")[:, 0:NB * SEQ].rearrange("p (b a d) -> p b a d", b=NB, d=DH)
                for r in range(2):
                    rows = slice(r * SEQ, (r + 1) * SEQ)
                    cp = act.copy(v_bd[c % 2][rows, :, :, r * VC:r * VC + DH], src[rows])
                cp.then_inc(free_misc("v"), 1)

            def keep_attn_t(c, p):
                act.wait_ge(attn_turned, TILES * c + p + 1)
                if p == 0:
                    wait(act, wo_made, c)
                act.copy(attn_t[:, p * P:(p + 1) * P], misc_of(f"out_t{p}")[:, 0:P]).then_inc(free_misc(f"out_t{p}"), 1)

            def keep_front(c):
                act.wait_ge(front_turned, c + 1)
                wait(act, v_made, c - 1)
                act.copy(front[c % 2][:].rearrange("p a t -> p (a t)"), misc_of("front_t")[:]).then_inc(free_misc("front_t"), 1)

            def hi_qk(c):
                act.wait_ge(qk_made, c + 1)
                wait(act, q_written, Q_WRITES * c)
                wait(act, k_written, K_WRITES * c)
                if c == 0:
                    act.wait_ge(in_b, 4 * DMA)
                for n, bias in enumerate((bq_c, bk_c)):
                    op = act.activation(parts[:, n, 0, :], misc_of("qk")[:, n * CH:(n + 1) * CH], ACT.Identity, bias=bias[:, 0:1])
                op.then_inc(qk_hi, 1)
                wait(act, qk_lo, c)
                for n, bias in enumerate((bq_c, bk_c)):
                    op = act.activation(qk_full[:, n, :], misc_of("qk")[:, n * CH:(n + 1) * CH], ACT.Identity, bias=bias[:, 0:1])
                op.then_inc(free_misc("qk"), 1)

            act.wait_ge(w_turned, 1)
            for n, w in enumerate((wq_t, wk_t)):
                act.copy(w[:].rearrange("p (h d g) -> p g h d", h=4, g=G),
                         ffn_ps[0][:, n * P:(n + 1) * P].rearrange("p (g h d) -> p g h d", g=G, h=4)).then_inc(w_kept, 1)
            for n, w in enumerate((wv_t, wo_t)):
                act.copy(w[:], ffn_ps[0][:, (n + 2) * P:(n + 3) * P]).then_inc(w_kept, 1)

            for i in range(turns):
                if live(i - 3):
                    keep_attn_t(i - 3, 1)
                if live(i - 2):
                    exp(i - 2, 1)
                if live(i):
                    keep_front(i)
                if live(i - 4):
                    hi_ffn(i - 4, 2)
                if live(i):
                    hi_qk(i)
                if live(i - 2):
                    exp(i - 2, 2)
                if live(i - 4):
                    hi_ffn(i - 4, 3)
                if live(i - 1):
                    keep_v(i - 1)
                if live(i - 2):
                    keep_attn_t(i - 2, 0)
                    exp(i - 2, 3)
                if live(i - 3):
                    act.wait_ge(xn2_turned, i - 2)
                    act.copy(xn2_t[:, 0, :], misc_of("xn2_t")[:, 0:CH]).then_inc(xn2_hi, 1)
                if closing(i):
                    hi_ffn(i - 3, 0)
                    hi_ffn(i - 3, 1)
                if live(i - 4):
                    act.wait_ge(yt_made, i - 3)
                    act.copy(y_t[:], misc_of("y_t")[:, 0:CH]).then_inc(free_misc("y_t"), 1)
                if live(i - 1):
                    exp(i - 1, 0)
                if live(i - 3) and not closing(i):
                    hi_ffn(i - 3, 0)
                    hi_ffn(i - 3, 1)

        @block.gpsimd
        def _(pool):
            pool.memset(ones[:], 1.0).then_inc(ones_made, 1)
            pool.wait_ge(ones_made, 1)
            pool.affine_select(out=ident[:], in_=ones[:], compare_op=ALU.is_equal, fill=0.0, base=0,
                               pattern=[[-1, P]], channel_multiplier=1).then_inc(ident_made, 1)
            pool.memset(minus_half[:], -0.5).then_inc(half_made, 1)
            pool.wait_ge(half_made, 1)

            def rstd(c, ve, rs, ve_done, rs_done):
                pool.wait_ge(ve_done, c + 1)
                pool.tensor_tensor(rs[:], ve[:], minus_half[:], ALU.pow).then_inc(rs_done, 1)

            rstd(0, ve1, rs1, ve1_done, rs1_done)

            pool.memset(k_st[0][:].bitcast(U32), 0).then_inc(k_zeroed, 1)

            for i in range(turns):
                if live(i - 3):
                    rstd(i - 3, ve2, rs2, ve2_done, rs2_done)
                if live(i + 1):
                    rstd(i + 1, ve1, rs1, ve1_done, rs1_done)
                if live(i - 4):
                    pool.wait_ge(h2_kept, i - 3)
                    pool.tensor_tensor(h2[:, 1, 0:2, :], h2_full[:], h2[:, 0, 0:2, :].bitcast(F32), ALU.subtract).then_inc(h2_lo, 1)
                if live(i):
                    kept(pool, "qk", i)
                    pool.tensor_tensor(parts[:, :, 1, :], qk_full[:], parts[:, :, 0, :].bitcast(F32), ALU.subtract).then_inc(qk_lo, 1)
                if live(i + 1):
                    normalise(pool, i + 1, xn, mv1, rs1, rs1_done, xn_done, front_turned)
                if live(i):
                    if i == 0:
                        pool.wait_ge(bo_kept, 1)
                    pool.wait_ge(xn_done, i + 1)
                    xa = x_all[:, tile(i, 0, TILES), :]
                    pool.tensor_tensor(xa, xa, bo_row[:].unsqueeze(1).broadcast_to([P, TILES, P]), ALU.add).then_inc(x_biased, 1)
                if i == 0:
                    pool.memset(k_st[1][:].bitcast(U32), 0).then_inc(k_zeroed, 1)

        @block.vector
        def _(dve):
            def stats(c, st, mv, ve, st_done, mv_done, ve_done):
                for t in range(TILES):
                    op = dve.bn_stats(st[:, t, :], x_all[:, c * TILES + t, :])
                op.then_inc(st_done, 1)
                dve.wait_ge(st_done, c + 1)
                for t in range(TILES):
                    op = dve.bn_aggr(mv[:, t, :], st[:, t, :])
                op.then_inc(mv_done, 1)
                dve.wait_ge(mv_done, c + 1)
                dve.tensor_scalar(ve[:], mv[:, :, 1], EPS, None, ALU.add).then_inc(ve_done, 1)

            def stats1(c):
                wait_load(dve, x_in, c)
                wait(dve, xn_done, c)
                stats(c, st1, mv1, ve1, st1_done, mv1_done, ve1_done)

            def shift(c, u):
                n = u % 2
                scores = score_ps[n][:].rearrange("p (a k) -> p a k", a=UH)
                dve.wait_ge(scores_made, UNITS * c + u + 1)
                dve.tensor_reduce(row_max[n][:], scores, AX.X, ALU.max).then_inc(max_made, 1)
                dve.wait_ge(max_made, UNITS * c + u + 1)
                wait(dve, scores_turned, UNITS * c + u - 1)
                dve.tensor_tensor(shifted[n][:].rearrange("p (a k) -> p a k", a=UH), scores,
                                  row_max[n][:].unsqueeze(2).broadcast_to([P, UH, SEQ]), ALU.subtract).then_inc(shift_done, 1)

            def lo_ffn(c, f):
                h = h1 if f < 2 else h2
                m = 2 * (f % 2)
                dve.wait_ge(ffn_hi, FT * c + f + 1)
                dve.scalar_tensor_tensor(out=h[:, 1, m:m + 2, :], in0=ffn_ps[f % 2][:].rearrange("p (m t) -> p m t", m=2), scalar=0.0,
                                         in1=h[:, 0, m:m + 2, :].bitcast(F32), op0=ALU.max, op1=ALU.subtract).then_inc(ffn_lo, 1)

            def normalise_attn(c, p):
                dve.wait_ge(pv_made, TILES * c + p + 1)
                wait(dve, attn_turned, TILES * (c - 1) + p + 1)
                o = misc_of(f"pv{p}")[:, 0:HP * OC].rearrange("p (a b r c) -> p b a r c", a=HP, b=2, r=2)
                for b in range(2):
                    rows = slice(b * SEQ, (b + 1) * SEQ)
                    op = dve.reciprocal(inv_den[p][rows], o[rows, b, :, :, DH])
                op.then_inc(den_done, 1)
                dve.wait_ge(den_done, TILES * c + p + 1)
                for b in range(2):
                    rows = slice(b * SEQ, (b + 1) * SEQ)
                    op = dve.tensor_tensor(attn[p][rows], o[rows, b, :, :, 0:DH],
                                           inv_den[p][rows].unsqueeze(3).broadcast_to([SEQ, HP, 2, DH]), ALU.mult)
                op.then_inc(free_misc(f"pv{p}"), 1)

            def add_attention(c):
                dve.wait_ge(wo_made, c + 1)
                dve.wait_ge(x_biased, c + 1)
                xa = x_all[:, tile(c, 0, TILES), :]
                dve.tensor_tensor(xa, misc_of("wo")[:, 0:CH].rearrange("p (t d) -> p t d", t=TILES), xa, ALU.add).then_inc(free_misc("wo"), 1)
                kept(dve, "wo", c)
                stats(c, st2, mv2, ve2, st2_done, mv2_done, ve2_done)

            stats1(0)
            normalise(dve, 0, xn, mv1, rs1, rs1_done, xn_done, front_turned)
            for n in range(2):
                dve.memset(v_bd[n][:], 0.0).then_inc(v_zeroed, 1)
            dve.wait_ge(v_zeroed, 2)
            for n in range(2):
                for r in range(2):
                    op = dve.memset(v_bd[n][r * SEQ:(r + 1) * SEQ, :, :, r * VC + DH:r * VC + DH + 1], 1.0)
            op.then_inc(v_ones, 1)
            dve.memset(q_st[0][:].bitcast(U32), 0).then_inc(q_zeroed, 1)
            dve.wait_ge(in_b, 4 * DMA)
            dve.wait_ge(ones_made, 1)
            dve.tensor_scalar(bv_rep[:], ones[:], bv_c[:, 0:1], None, ALU.mult).then_inc(bv_made, 1)

            def setup_ffn():
                dve.wait_ge(in_s, 3 * DMA)
                dve.wait_ge(in_k, 3 * DMA)
                dve.tensor_scalar(s_pos[:], s_raw[:], 0.0, None, ALU.is_gt)
                dve.tensor_scalar(s_neg[:], s_raw[:], 0.0, None, ALU.is_lt).then_inc(scale_step, 1)
                dve.wait_ge(scale_step, 1)
                dve.tensor_tensor(s_sgn[:], s_pos[:], s_neg[:], ALU.subtract)
                dve.tensor_tensor(k0_diff[:], k0_sb[:, 0, :], k0_sb[:, 1, :], ALU.subtract).then_inc(scale_step, 1)
                dve.wait_ge(scale_step, 2)
                dve.tensor_scalar(s_sgn2[:], s_sgn[:], 2.0, None, ALU.mult)
                dve.tensor_scalar(s_nsgn[:], s_sgn[:], -1.0, None, ALU.mult)
                dve.tensor_tensor(s_abs[:], s_raw[:], s_sgn[:], ALU.mult).then_inc(scale_step, 1)
                dve.wait_ge(scale_step, 3)
                dve.tensor_scalar(w0[:], k0_diff[:], s_sgn2[:, 0:1], None, ALU.mult)
                dve.tensor_scalar(w1[:], k1_sb[:], s_sgn2[:, 1:2], s_nsgn[:, 1:2], ALU.mult, ALU.add)
                dve.tensor_scalar(w2[:], k2_sb[:], 2.0, -1.0, ALU.mult, ALU.add)
                dve.tensor_tensor(s_01[:], s_abs[:, 0:1], s_abs[:, 1:2], ALU.mult).then_inc(scale_step, 1)
                dve.wait_ge(scale_step, 4)
                dve.tensor_scalar(s_01x4[:], s_01[:], 4.0, None, ALU.mult).then_inc(scale_step, 1)
                dve.wait_ge(scale_step, 5)
                dve.tensor_tensor(s_fin[:], s_01x4[:], s_raw[:, 2:3], ALU.mult).then_inc(ffn_w_made, 1)
                dve.wait_ge(ffn_w_made, 1)

            for i in range(turns):
                if live(i - 2):
                    shift(i - 2, 2)
                if live(i - 3):
                    add_attention(i - 3)
                if live(i + 1):
                    stats1(i + 1)
                if i == 0:
                    dve.memset(q_st[1][:].bitcast(U32), 0).then_inc(q_zeroed, 1)
                if live(i - 3):
                    normalise(dve, i - 3, xn2, mv2, rs2, rs2_done, xn2_done, xn2_turned)
                if live(i - 2):
                    shift(i - 2, 3)
                if live(i - 2):
                    normalise_attn(i - 2, 0)
                if live(i - 4):
                    lo_ffn(i - 4, 3)
                if live(i - 1):
                    shift(i - 1, 0)
                if i == 0:
                    dve.wait_ge(bo_made, 1)
                    dve.tensor_tensor(bo_row[:], ffn_ps[1][:, 0:P], bo_row[:], ALU.add).then_inc(bo_kept, 1)
                    setup_ffn()
                if live(i - 3):
                    dve.wait_ge(xn2_hi, i - 2)
                    dve.tensor_tensor(xn2_t[:, 1, :], misc_of("xn2_t")[:, 0:CH], xn2_t[:, 0, :].bitcast(F32), ALU.subtract).then_inc(free_misc("xn2_t"), 1)
                if live(i - 1):
                    shift(i - 1, 1)
                if live(i - 2):
                    normalise_attn(i - 2, 1)
                if closing(i):
                    lo_ffn(i - 3, 0)
                    lo_ffn(i - 3, 1)
                if live(i - 4):
                    dve.wait_ge(y_made, i - 3)
                    xa = x_all[:, tile(i - 4, 0, TILES), :]
                    dve.scalar_tensor_tensor(out=xa, in0=misc_of("y")[:, 0:CH].rearrange("p (t d) -> p t d", t=TILES), scalar=s_fin[:, 0:1], in1=xa,
                                             op0=ALU.mult, op1=ALU.add).then_inc(free_misc("y"), 1)
                if live(i - 3) and not closing(i):
                    lo_ffn(i - 3, 0)
                    lo_ffn(i - 3, 1)
    return nc


_INS = ['x', 'ctx_1024', 'L0_xattn_w_q', 'L0_xattn_b_q', 'L0_xattn_w_k', 'L0_xattn_b_k', 'L0_xattn_w_v', 'L0_xattn_b_v',
        'L0_xattn_w_o', 'L0_xattn_b_o', 'L0_ffn_k0', 'L0_ffn_k1', 'L0_ffn_k2', 'L0_ffn_s0', 'L0_ffn_s1', 'L0_ffn_s2']


def kernel(**inputs):
    import numpy as _np
    import concourse.bacc as _bacc
    from concourse import mybir as _mybir
    from concourse.bass_utils import run_bass_kernel_spmd as _run

    nc = _bacc.Bacc("TRN2", target_bir_lowering=False, num_devices=1)
    arrays, args = {}, []
    for name in _INS:
        a = _np.ascontiguousarray(inputs[name])
        if a.ndim == 0:
            a = a.reshape(1)
        arrays[f"in_{name}_dram"] = a
        args.append(nc.dram_tensor(f"in_{name}_dram", a.shape, _mybir.dt.from_np(a.dtype), kind="ExternalInput").ap())
    shape = tuple(_np.shape(inputs['x']))
    args.append(nc.dram_tensor("out_0_dram", shape, _mybir.dt.float32, kind="ExternalOutput").ap())
    program(nc, *args)
    r = _run(nc, [arrays], core_ids=[0])
    return r.results[0]["out_0_dram"]
```
